# Optimizing a Trainium2 kernel written in Bass

```python
import numpy as np
import jax
import jax.numpy as jnp

def _softmax(x, axis=-1):
    return jax.nn.softmax(x, axis=axis)

def _gelu(x):
    return jax.nn.gelu(x, approximate=True)

def _silu(x):
    return jax.nn.silu(x)

def _sigmoid(x):
    return jax.nn.sigmoid(x)

def _layernorm(x, axis=-1, eps=1e-05):
    m = jnp.mean(x, axis=axis, keepdims=True)
    v = jnp.var(x, axis=axis, keepdims=True)
    return (x - m) / jnp.sqrt(v + eps)

def _scatter_add(tgt, idx, src, axis=0):
    return tgt.at[idx].add(src)

def _segment_sum(src, seg, n):
    return jax.ops.segment_sum(src, seg, n)
kernel_name = 'mk_conv_preact_d4_conv_nchw64_r2_3c5e35'

def setup_inputs(seed: int=0):
    np.random.seed(seed)
    _w = jnp.asarray

    def _rec_inputs():
        import jax
        import jax.numpy as jnp
        _gk = jax.random.key(seed)
        x = -0.000929 + 1 * jax.random.normal(jax.random.fold_in(_gk, 1), (4, 32, 32, 32), jnp.float32)
        return x
    x = _rec_inputs()

    def _L0_conv_setup():
        import jax, jax.numpy as jnp
        import numpy as np
        import itertools
        K = 3
        KSS = K * K
        STRIDE = 1
        PAD = 1
        ORDERS = (1, 2)

        def _unfold(x, k, stride, pad):
            B, C, H, W = x.shape
            xp = jnp.pad(x, ((0, 0), (0, 0), (pad, pad), (pad, pad)))
            oh = (H + 2 * pad - k) // stride + 1
            ow = (W + 2 * pad - k) // stride + 1
            rows = (jnp.arange(oh) * stride)[:, None] + jnp.arange(k)[None, :]
            cols = (jnp.arange(ow) * stride)[:, None] + jnp.arange(k)[None, :]
            p = xp[:, :, rows[:, None, :, None], cols[None, :, None, :]]
            p = p.transpose(0, 1, 4, 5, 2, 3).reshape(B, C * k * k, oh * ow)
            return (p, oh, ow)

        def _superdiag_keep(kss, order):
            keep = np.zeros((kss,) * order, dtype=bool)
            for idx in itertools.combinations_with_replacement(range(kss), order):
                keep[idx] = True
            return keep.reshape(-1)

        def _volterra_features(xp4, order):
            if order == 1:
                return xp4
            f = xp4
            for _ in range(order - 1):
                f = jnp.einsum('bclp,bclq->bclpq', f, xp4)
                f = f.reshape(*f.shape[:3], -1)
            keep = _superdiag_keep(KSS, order)
            scale = 1.0 / np.sqrt(keep.sum())
            return f * jnp.asarray(keep, f.dtype) * jnp.asarray(scale, f.dtype)
        key = jax.random.key(seed)
        k1, k2, k3 = jax.random.split(key, 3)
        B, C, H, W = (4, 32, 32, 32)
        out_ch = 32
        x = jax.random.normal(k1, (B, C, H, W), dtype=jnp.float32)
        W1 = jax.random.normal(k2, (C * KSS, out_ch), dtype=jnp.float32) * 0.05
        W2 = jax.random.normal(k3, (C * KSS ** 2, out_ch), dtype=jnp.float32) * 0.02
        bias_w = jnp.zeros((out_ch, 1, 1), dtype=jnp.float32)
        return {'x': x, 'W1': W1, 'W2': W2, 'bias_w': bias_w}
    _L0_conv_all = _L0_conv_setup()
    _L0_conv_in = {k: v for k, v in _L0_conv_all.items() if k in ('W1', 'W2', 'bias_w')}
    del _L0_conv_all

    def _L1_conv_setup():
        import jax, jax.numpy as jnp
        import numpy as np
        B, CIN, COUT, H, W = (16, 32, 32, 64, 64)
        KH, KW = (3, 3)
        PAD, STRIDE = (1, 1)
        key = jax.random.key(seed)
        k1, k2 = jax.random.split(key)
        x = jax.random.normal(k1, (B, CIN, H, W), dtype=jnp.float32)
        scale = (1.0 / (CIN * KH * KW)) ** 0.5
        weight = jax.random.normal(k2, (COUT, CIN, KH, KW), dtype=jnp.float32) * scale
        bias = jnp.zeros((COUT,), dtype=jnp.float32)
        return {'x': x, 'weight': weight, 'bias': bias}
    _L1_conv_all = _L1_conv_setup()
    _L1_conv_in = {k: v for k, v in _L1_conv_all.items() if k in ('weight', 'bias')}
    del _L1_conv_all

    def _L2_conv_setup():
        import jax, jax.numpy as jnp
        import numpy as np
        N, I = (4, 32)
        CR, CA, CO = (32, 32, 32)
        HEADS, S = (4, 3)
        HC = CA // HEADS
        H, W = (48, 48)
        INIT_I, INIT_F = (-1.0, 1.0)

        def _conv(x, w, padding):
            return jax.lax.conv_general_dilated(x, w, window_strides=(1, 1), padding=padding, dimension_numbers=('NCHW', 'OIHW', 'NCHW'))
        key = jax.random.key(seed)
        ks = jax.random.split(key, 8)
        std = 0.05
        x = jax.random.normal(ks[0], (N, I, H, W), jnp.float32)
        W_in = jax.random.normal(ks[1], (CR, I), jnp.float32) * std
        b_in = jnp.zeros((CR,), jnp.float32)
        Wq = jax.random.normal(ks[2], (4, CA, CR, S, S), jnp.float32) * std * HC ** (-0.5)
        Wk = jax.random.normal(ks[3], (4, CA, CR, S, S), jnp.float32) * std
        Wv = jax.random.normal(ks[4], (4, CA, CR, S, S), jnp.float32) * std
        Wproj = jax.random.normal(ks[5], (4, 4, CR, CA), jnp.float32) * std * 0.5
        b_gates = jnp.array([INIT_I, INIT_F, 0.0, 0.0], jnp.float32)[:, None] * jnp.ones((4, CR), jnp.float32)
        W_out = jax.random.normal(ks[6], (CO, CR), jnp.float32) * std
        b_out = jnp.zeros((CO,), jnp.float32)
        return {'x': x, 'W_in': W_in, 'b_in': b_in, 'Wq': Wq, 'Wk': Wk, 'Wv': Wv, 'Wproj': Wproj, 'b_gates': b_gates, 'W_out': W_out, 'b_out': b_out}
    _L2_conv_all = _L2_conv_setup()
    _L2_conv_in = {k: v for k, v in _L2_conv_all.items() if k in ('W_in', 'b_in', 'Wq', 'Wk', 'Wv', 'Wproj', 'b_gates', 'W_out', 'b_out')}
    del _L2_conv_all

    def _L3_conv_setup():
        import jax, jax.numpy as jnp
        import numpy as np
        MODES1, MODES2 = (32, 32)

        def fht_matrix(N):
            if N == 1:
                return np.ones((1, 1), np.float32)
            M = fht_matrix(N // 2)
            k = np.arange(N // 2)
            cas = (np.cos(2 * np.pi * k / N) + np.sin(2 * np.pi * k / N)).astype(np.float32)[:, None]
            E = np.zeros((N // 2, N), np.float32)
            E[:, 0::2] = M
            O = np.zeros((N // 2, N), np.float32)
            O[:, 1::2] = M
            return np.concatenate([E + cas * O, E - cas * O], axis=0)

        def dht2(x, M1, M2):
            return jnp.einsum('bchw,kh,lw->bckl', x, M1, M2)

        def neg_freq(a):
            return jnp.roll(jnp.flip(a, axis=(-2, -1)), shift=(1, 1), axis=(-2, -1))

        def compl_mul2d(x1, x2):
            x1n = neg_freq(x1)
            x2n = neg_freq(x2)
            return 0.5 * (jnp.einsum('bixy,ioxy->boxy', x1, x2) - jnp.einsum('bixy,ioxy->boxy', x1n, x2n) + jnp.einsum('bixy,ioxy->boxy', x1, x2n) + jnp.einsum('bixy,ioxy->boxy', x1n, x2))
        key = jax.random.key(seed)
        k1, k2 = jax.random.split(key)
        B, Cin, Cout, S = (32, 32, 32, 64)
        x = jax.random.normal(k1, (B, Cin, S, S), jnp.float32)
        scale = 1.0 / (Cin * Cout)
        weights1 = scale * jax.random.uniform(k2, (Cin, Cout, MODES1, MODES2), jnp.float32)
        return {'x': x, 'weights1': weights1}
    _L3_conv_all = _L3_conv_setup()
    _L3_conv_in = {k: v for k, v in _L3_conv_all.items() if k in ('weights1',)}
    del _L3_conv_all
    return {'x': x, 'L0_conv_W1': _L0_conv_in['W1'], 'L0_conv_W2': _L0_conv_in['W2'], 'L0_conv_bias_w': _L0_conv_in['bias_w'], 'L1_conv_weight': _L1_conv_in['weight'], 'L1_conv_bias': _L1_conv_in['bias'], 'L2_conv_W_in': _L2_conv_in['W_in'], 'L2_conv_b_in': _L2_conv_in['b_in'], 'L2_conv_Wq': _L2_conv_in['Wq'], 'L2_conv_Wk': _L2_conv_in['Wk'], 'L2_conv_Wv': _L2_conv_in['Wv'], 'L2_conv_Wproj': _L2_conv_in['Wproj'], 'L2_conv_b_gates': _L2_conv_in['b_gates'], 'L2_conv_W_out': _L2_conv_in['W_out'], 'L2_conv_b_out': _L2_conv_in['b_out'], 'L3_conv_weights1': _L3_conv_in['weights1']}

def reference(x, L0_conv_W1, L0_conv_W2, L0_conv_bias_w, L1_conv_weight, L1_conv_bias, L2_conv_W_in, L2_conv_b_in, L2_conv_Wq, L2_conv_Wk, L2_conv_Wv, L2_conv_Wproj, L2_conv_b_gates, L2_conv_W_out, L2_conv_b_out, L3_conv_weights1):
    import jax
    import jax.numpy as jnp

    def _L0_conv_ref(x, W1, W2, bias_w):
        import jax, jax.numpy as jnp
        import numpy as np
        import itertools
        K = 3
        KSS = K * K
        STRIDE = 1
        PAD = 1
        ORDERS = (1, 2)

        def _unfold(x, k, stride, pad):
            B, C, H, W = x.shape
            xp = jnp.pad(x, ((0, 0), (0, 0), (pad, pad), (pad, pad)))
            oh = (H + 2 * pad - k) // stride + 1
            ow = (W + 2 * pad - k) // stride + 1
            rows = (jnp.arange(oh) * stride)[:, None] + jnp.arange(k)[None, :]
            cols = (jnp.arange(ow) * stride)[:, None] + jnp.arange(k)[None, :]
            p = xp[:, :, rows[:, None, :, None], cols[None, :, None, :]]
            p = p.transpose(0, 1, 4, 5, 2, 3).reshape(B, C * k * k, oh * ow)
            return (p, oh, ow)

        def _superdiag_keep(kss, order):
            keep = np.zeros((kss,) * order, dtype=bool)
            for idx in itertools.combinations_with_replacement(range(kss), order):
                keep[idx] = True
            return keep.reshape(-1)

        def _volterra_features(xp4, order):
            if order == 1:
                return xp4
            f = xp4
            for _ in range(order - 1):
                f = jnp.einsum('bclp,bclq->bclpq', f, xp4)
                f = f.reshape(*f.shape[:3], -1)
            keep = _superdiag_keep(KSS, order)
            scale = 1.0 / np.sqrt(keep.sum())
            return f * jnp.asarray(keep, f.dtype) * jnp.asarray(scale, f.dtype)
        B, C, H, W = x.shape
        unf, oh, ow = _unfold(x, K, STRIDE, PAD)
        L = oh * ow
        xp4 = unf.reshape(B, C, KSS, L).transpose(0, 1, 3, 2)
        out = 0.0
        for order, Wt in zip(ORDERS, (W1, W2)):
            f = _volterra_features(xp4, order)
            feat = f.transpose(0, 2, 1, 3).reshape(B, L, -1)
            out = out + feat @ Wt
        out_ch = W1.shape[1]
        out = out.reshape(B, out_ch, oh, ow) + bias_w
        return out

    def _L1_conv_ref(x, weight, bias):
        import jax, jax.numpy as jnp
        import numpy as np
        B, CIN, COUT, H, W = (16, 32, 32, 64, 64)
        KH, KW = (3, 3)
        PAD, STRIDE = (1, 1)
        b, c, h, w = x.shape
        kh, kw = (weight.shape[2], weight.shape[3])
        pad_h = h + kh - 1
        pad_w = w + kw - 1
        x_padded = jnp.pad(x, ((0, 0), (0, 0), (0, pad_h - h), (0, pad_w - w)))
        w_padded = jnp.pad(weight, ((0, 0), (0, 0), (0, pad_h - kh), (0, pad_w - kw)))
        X_fft = jnp.fft.rfft2(x_padded)
        W_fft = jnp.fft.rfft2(w_padded, s=(pad_h, pad_w))
        Y_fft = jnp.einsum('bchw,oihw->bohw', X_fft, W_fft)
        y = jnp.fft.irfft2(Y_fft, s=(pad_h, pad_w))
        y = y[:, :, PAD:-PAD:STRIDE, PAD:-PAD:STRIDE]
        y = y + bias[None, :, None, None]
        return y

    def _L2_conv_ref(x, W_in, b_in, Wq, Wk, Wv, Wproj, b_gates, W_out, b_out):
        import jax, jax.numpy as jnp
        import numpy as np
        N, I = (4, 32)
        CR, CA, CO = (32, 32, 32)
        HEADS, S = (4, 3)
        HC = CA // HEADS
        H, W = (48, 48)
        INIT_I, INIT_F = (-1.0, 1.0)

        def _conv(x, w, padding):
            return jax.lax.conv_general_dilated(x, w, window_strides=(1, 1), padding=padding, dimension_numbers=('NCHW', 'OIHW', 'NCHW'))
        n, _, hh, ww = x.shape
        xin = jnp.einsum('nchw,oc->nohw', x, W_in) + b_in[None, :, None, None]
        h = jnp.zeros_like(xin)
        pairs = ((xin, xin), (xin, h), (h, xin), (h, h))
        attns = []
        for idx, (query, token) in enumerate(pairs):
            q = _conv(query, Wq[idx], 'SAME').reshape(n, HEADS, HC, -1)
            k = _conv(token, Wk[idx], 'VALID').reshape(n, HEADS, HC, -1)
            v = _conv(token, Wv[idx], 'VALID').reshape(n, HEADS, HC, -1)
            w = jax.nn.softmax(jnp.einsum('nhcq,nhcd->nhqd', q, k), axis=-1)
            a = jnp.einsum('nhcd,nhqd->nhcq', v, w).reshape(n, CA, hh, ww)
            attns.append(a)
        A = jnp.stack(attns, axis=0)
        pre = jnp.einsum('anchw,gaoc->gnohw', A, Wproj) + b_gates[:, None, :, None, None]
        i = jax.nn.sigmoid(pre[0])
        f = jax.nn.sigmoid(pre[1])
        g = jnp.tanh(pre[2])
        o = jax.nn.sigmoid(pre[3])
        c = i * g
        hout = o * jnp.tanh(c)
        return jnp.einsum('nchw,oc->nohw', hout, W_out) + b_out[None, :, None, None]

    def _L3_conv_ref(x, weights1):
        import jax, jax.numpy as jnp
        import numpy as np
        MODES1, MODES2 = (32, 32)

        def fht_matrix(N):
            if N == 1:
                return np.ones((1, 1), np.float32)
            M = fht_matrix(N // 2)
            k = np.arange(N // 2)
            cas = (np.cos(2 * np.pi * k / N) + np.sin(2 * np.pi * k / N)).astype(np.float32)[:, None]
            E = np.zeros((N // 2, N), np.float32)
            E[:, 0::2] = M
            O = np.zeros((N // 2, N), np.float32)
            O[:, 1::2] = M
            return np.concatenate([E + cas * O, E - cas * O], axis=0)

        def dht2(x, M1, M2):
            return jnp.einsum('bchw,kh,lw->bckl', x, M1, M2)

        def neg_freq(a):
            return jnp.roll(jnp.flip(a, axis=(-2, -1)), shift=(1, 1), axis=(-2, -1))

        def compl_mul2d(x1, x2):
            x1n = neg_freq(x1)
            x2n = neg_freq(x2)
            return 0.5 * (jnp.einsum('bixy,ioxy->boxy', x1, x2) - jnp.einsum('bixy,ioxy->boxy', x1n, x2n) + jnp.einsum('bixy,ioxy->boxy', x1, x2n) + jnp.einsum('bixy,ioxy->boxy', x1n, x2))
        B, Cin, S1, S2 = x.shape
        Cout = weights1.shape[1]
        M1 = jnp.asarray(fht_matrix(S1))
        M2 = jnp.asarray(fht_matrix(S2))
        x_ht = dht2(x, M1, M2)
        block = compl_mul2d(x_ht[:, :, :MODES1, :MODES2], weights1)
        out_ht = jnp.zeros((B, Cout, S1, S2), x.dtype).at[:, :, :MODES1, :MODES2].set(block)
        return dht2(out_ht, M1, M2) / (S1 * S2)

    def _gn(v, G=32, eps=1e-05):
        B_, C_, H_, W_ = v.shape
        g = v.reshape(B_, G, C_ // G, H_, W_)
        m = jnp.mean(g, axis=(2, 3, 4), keepdims=True)
        s = jnp.var(g, axis=(2, 3, 4), keepdims=True)
        return ((g - m) / jnp.sqrt(s + eps)).reshape(v.shape)

    def _ln_c(v, eps=1e-06):
        m = jnp.mean(v, axis=1, keepdims=True)
        s = jnp.var(v, axis=1, keepdims=True)
        return (v - m) / jnp.sqrt(s + eps)

    def _ln_t(v, eps=1e-05):
        m = jnp.mean(v, axis=-1, keepdims=True)
        s = jnp.var(v, axis=-1, keepdims=True)
        return (v - m) / jnp.sqrt(s + eps)

    def _to_tokens(v):
        B_, C_, H_, W_ = v.shape
        return v.reshape(B_, C_, H_ * W_).transpose(0, 2, 1)

    def _from_tokens(t, like):
        B_, C_, H_, W_ = like.shape
        return t.transpose(0, 2, 1).reshape(B_, C_, H_, W_)
    x = x + _L0_conv_ref(_gn(x), L0_conv_W1, L0_conv_W2, L0_conv_bias_w)
    x = x + _L1_conv_ref(_gn(x), L1_conv_weight, L1_conv_bias)
    x = x + _L2_conv_ref(_gn(x), L2_conv_W_in, L2_conv_b_in, L2_conv_Wq, L2_conv_Wk, L2_conv_Wv, L2_conv_Wproj, L2_conv_b_gates, L2_conv_W_out, L2_conv_b_out)
    x = x + _L3_conv_ref(_gn(x), L3_conv_weights1)
    return x

_drawn_inputs = setup_inputs


def setup_inputs(seed=0):
    import zlib

    import numpy as np

    out = dict(_drawn_inputs(seed))
    spreads = {'L0_conv_bias_w': (0.0, 0.292),
     'L1_conv_bias': (0.0, 0.44),
     'L2_conv_b_in': (0.0, 0.8),
     'L2_conv_b_out': (0.0, 0.411)}
    factors = {'L2_conv_W_in': 8.0,
     'L2_conv_Wq': 8.0,
     'L2_conv_Wk': 8.0,
     'L2_conv_Wv': 8.0,
     'L2_conv_Wproj': 8.0,
     'L2_conv_b_gates': 7.395,
     'L2_conv_W_out': 8.0,
     'L3_conv_weights1': 187.95}
    for name, (base, spread) in spreads.items():
        noise = np.random.default_rng([zlib.crc32(name.encode()), seed]).standard_normal(out[name].shape)
        drawn = base * np.exp(spread * noise) if base else spread * noise
        out[name] = jnp.asarray(drawn.astype(out[name].dtype))
    for name, factor in factors.items():
        out[name] = (out[name] * factor).astype(out[name].dtype)
    return out
```

```python
from contextlib import ExitStack

import numpy as np

import concourse.bass as bass
from concourse import mybir

F32 = mybir.dt.float32
BF16 = mybir.dt.bfloat16
I32 = mybir.dt.int32
ACT = mybir.ActivationFunctionType
ALU = mybir.AluOpType
AX = mybir.AxisListType

P = 128
B, C, H, W = 4, 32, 32, 32
HW = H * W
HALF = HW // 2
WP = W + 2
NP = WP * WP
XPW = NP + 76
EPS = 1e-5

LINEAR = None
TILES = [
    [(LINEAR, 0), ((0, 0), 0), ((0, 1), 0), ((1, 0), 0)],
    [((1, 1), 0), ((1, -1), 1), ((0, 2), 0), ((2, 0), 0)],
    [((1, 2), 0), ((1, -2), 2), ((2, 1), 0), ((2, -1), 1)],
]
SINGLES = [((2, 2), (0, 0)), ((2, -2), (0, 2))]
MAPS = [d for d, _ in SINGLES] + [d for tile in TILES for d, _ in tile if d is not LINEAR]
MAPW = NP + 2


def tap_pair(d, pre, py, px):
    dy, dx = d or (0, 0)
    px = px + pre
    qy, qx = py + dy, px + dx
    if px > 2 or not (0 <= qy <= 2 and 0 <= qx <= 2):
        return None
    return py * 3 + px, qy * 3 + qx


SLOTS = [(t, (py, px)) for t, tile in enumerate(TILES) for py in range(3) for px in range(3)
         if any(tap_pair(d, pre, py, px) for d, pre in tile)]
N_KEPT = 45
VOLTERRA_SCALE = float(np.float32(1.0 / np.sqrt(N_KEPT)))

HEADS, HC = 4, 8
G = B * HEADS
KH = H - 2
KEYS = KH * KH
KHALF = KEYS // 2
DT = KEYS // P
KREST = KEYS - DT * P
KPAD = DT * P + 32
PARTS = 3
PAIR_ROWS = PARTS * PARTS * HC
S_ROWS = PAIR_ROWS + PARTS
QT_TILES = HW // P
MAX_UNITS = HEADS * QT_TILES * 2
MU = MAX_UNITS + 1
EXP_UNITS = HEADS * DT + 1
PRING = 16
GATES = (0, 2, 3)
MODES = 32
KG = MODES // 4

CONSTS = {}


def _place(names):
    at = 0
    for name, n in names:
        CONSTS[name] = (at, n)
        at += n
    return at


N_FIRST = _place([("l0w", len(SLOTS) * 32), ("l0single", 2 * P), ("l0bias", 1)])
N_CONST = N_FIRST
for _name, _n in [("l1w", 3 * 32), ("l1bias", 1), ("win", P), ("bin", 1), ("qkv", 3 * 3 * 32),
                  ("v2w", 9 * 32), ("proj", 3 * 32), ("proj2", 3 * 32), ("ones", P), ("gbias", 3), ("wout", P),
                  ("bout", 1), ("ident", P), ("mt", P), ("mrt", P), ("mnt", P)]:
    CONSTS[_name] = (N_CONST, _n)
    N_CONST += _n


def build(nc, x, consts, wmodes, out):
    ctx = ExitStack()
    with ctx:
        def sb(name, shape, dt=F32):
            return ctx.enter_context(nc.sbuf_tensor(name, shape, dt))

        def sem(name):
            return ctx.enter_context(nc.semaphore(name))

        xa = sb("xa", [P, HW])
        xb = sb("xb", [P, HW])
        xc = sb("xc", [P, HW])
        xp = sb("xp", [P, XPW])
        cst = sb("cst", [P, N_CONST])
        stats = sb("stats", [P, 12])
        small = sb("small", [P, 16])
        arena_a = sb("arena_a", [P, 15744])
        arena_b = sb("arena_b", [P, 16384])
        vt = sb("vt", [P, DT, G, 32])
        vrest = sb("vrest", [P, B, P])
        attn = sb("attn", [P, B, HW])
        ot = sb("ot", [P, 2, HALF])
        on = sb("on", [P, 2, HALF])
        rden = sb("rden", [P, 2, 16])
        mx = sb("mx", [P, MAX_UNITS])
        negm = sb("negm", [P, 2, MAX_UNITS // 2])
        mparts = sb("mparts", [P, PARTS, MAX_UNITS // 2], BF16)
        mt_sb = sb("mt_sb", [PARTS * MAX_UNITS // 2, P], BF16)
        ident_b = sb("ident_b", [P, P], BF16)
        wsum = sb("wsum", [P, 3, H])
        win9 = sb("win9", [P, 9])
        a2 = sb("a2", [P, 1])
        l1s = sb("l1s", [96, 3 * 32])
        gb = sb("gb", [P, 3])

        def c_(name, r0=0, r1=P):
            at, n = CONSTS[name]
            return cst[r0:r1, at:at + n]

        maps = arena_a[:, 0:len(MAPS) * MAPW].rearrange("p (m n) -> p m n", n=MAPW)
        q_words = G * HW // 2
        k_words = G * KPAD // 2
        qst = arena_a[:, 0:q_words].bitcast(BF16).rearrange("p (g n) -> p g n", g=G)
        kst = arena_a[:, q_words:q_words + k_words].bitcast(BF16).rearrange("p (g n) -> p g n", g=G)
        xm = arena_a[:, 0:8192].rearrange("p (n m) -> p n m", m=32)
        tmp3 = arena_a[:, 8192:8192 + 6 * HW].rearrange("p (t n) -> p t n", n=HW)
        stack = arena_b[:, 0:3 * B * NP].rearrange("p (t b n) -> p t b n", t=3, b=B)
        resid = arena_b[:, 0:2 * HW].rearrange("p (t n) -> p t n", t=2)
        probs = arena_b[:, 0:PRING * HALF].rearrange("p (s n) -> p s n", n=HALF)
        wm = arena_b[:, 8192:16384]
        y1 = arena_b[:, 0:2 * HW]
        z1 = arena_b[:, 2 * HW:4 * HW]
        qkparts = sb("qkparts", [P, 2, PARTS, HW], BF16)
        vs = arena_b[:, 2 * HW:2 * HW + KEYS]

        ps = ctx.enter_context(nc.psum_tensor("ps", [P, 8, 512], F32))

        def banks(i, n=2):
            return ps[:, i:i + n, :].rearrange("p a n -> p (a n)")

        q_dram = nc.dram_tensor("q_scratch", [P, PARTS, HW], BF16, kind="Internal").ap()
        k_dram = nc.dram_tensor("k_scratch", [P, PARTS, KEYS], BF16, kind="Internal").ap()
        m_dram = nc.dram_tensor("m_scratch", [B, PARTS * MAX_UNITS // 2, P], BF16, kind="Internal").ap()

        x_loaded = sem("x_loaded")
        first_loaded = sem("first_loaded")
        consts_loaded = sem("consts_loaded")
        wm_loaded = sem("wm_loaded")
        dve_step = sem("dve_step")
        padded = sem("padded")
        xp_zeroed = sem("xp_zeroed")
        map_ready = sem("map_ready")
        tile_hw = [sem(f"tile_hw{t}") for t in range(3)]
        tile_sw = [sem(f"tile_sw{t}") for t in range(3)]
        rep_hw = [sem(f"rep_hw{t}") for t in range(2)]
        rep_sw = [sem(f"rep_sw{t}") for t in range(2)]
        l0_done = sem("l0_done")
        l0_read = sem("l0_read")
        l1s_done = sem("l1s_done")
        l1s_ready = sem("l1s_ready")
        l1_done = sem("l1_done")
        l1_read = sem("l1_read")
        xn2_ready = sem("xn2_ready")
        xin_done = sem("xin_done")
        q_done = sem("q_done")
        k_done = sem("k_done")
        v_done = sem("v_done")
        part_act = sem("part_act")
        part_dve = sem("part_dve")
        vs_ready = sem("vs_ready")
        vt_done = sem("vt_done")
        vt_ready = sem("vt_ready")
        vt_zeroed = sem("vt_zeroed")
        win_ready = sem("win_ready")
        a2_done = sem("a2_done")
        a2_ready = sem("a2_ready")
        gb_done = sem("gb_done")
        gb_ready = sem("gb_ready")
        qd_written = sem("qd_written")
        kd_written = sem("kd_written")
        k_filled = sem("k_filled")
        q_in = [sem("q_in0"), sem("q_in1")]
        k_in = [sem("k_in0"), sem("k_in1")]
        max_scored = sem("max_scored")
        max_read = sem("max_read")
        m_split = sem("m_split")
        mt_copied = sem("mt_copied")
        md_written = sem("md_written")
        m_in = sem("m_in")
        scored = sem("scored")
        expd = sem("expd")
        pv_done = sem("pv_done")
        o_read = sem("o_read")
        o_scaled = sem("o_scaled")
        attn_ready = sem("attn_ready")
        gate_done = sem("gate_done")
        gate_act = sem("gate_act")
        cell_ready = sem("cell_ready")
        cell_act = sem("cell_act")
        h_ready = sem("h_ready")
        wout_done = sem("wout_done")
        x3_ready = sem("x3_ready")
        xm_zeroed = sem("xm_zeroed")
        t1_ready = sem("t1_ready")
        rows_done = sem("rows_done")
        t2_ready = sem("t2_ready")
        cols_done = sem("cols_done")
        tu_ready = sem("tu_ready")
        xm_dve = sem("xm_dve")
        xm_pool = sem("xm_pool")
        mix_done = sem("mix_done")
        y1_ready = sem("y1_ready")
        inv_l_done = sem("inv_l_done")
        z1_ready = sem("z1_ready")
        inv_k_done = sem("inv_k_done")
        res_ready = sem("res_ready")
        stored = sem("stored")

        block = ctx.enter_context(nc.Block())

        def interior(ap):
            return ap[:, WP + 1:WP + 1 + 32 * WP].rearrange("p (y x) -> p y x", x=WP)[:, :, 0:W]

        def window(image, py, px, y0, ny, nx):
            rows = image[:, (y0 + py) * WP:(y0 + py + ny) * WP].rearrange("p (y x) -> p y x", x=WP)
            return rows[:, :, px:px + nx]

        def by_pool(t, slot):
            return slot == 3 or (slot == 2 and t > 0)

        pool_tiles = [sum(by_pool(t, s) for s in range(4)) for t in range(3)]

        def map_index(t, slot):
            return MAPS.index(TILES[t][slot][0])

        def copy_slot(queue, t, slot, signal):
            d, pre = TILES[t][slot]
            if d is LINEAR:
                queue.wait_ge(padded, 1)
            else:
                queue.wait_ge(map_ready, map_index(t, slot) + 1)
            for b in range(B):
                rows = slice(32 * b, 32 * b + 32)
                src = xp[rows, 0:NP] if d is LINEAR else maps[rows, map_index(t, slot), pre:pre + NP]
                queue.dma_start(stack[32 * slot:32 * slot + 32, t, b, :], src).then_inc(signal, 16)

        def replicate(queue, layer, r, signal):
            for b in range(B):
                queue.dma_start(stack[32 * r:32 * r + 32, layer - 1, b, :],
                                xp[32 * b:32 * b + 32, WP * r:WP * r + NP]).then_inc(signal, 16)

        def gather_parts(queue, what, images, signal):
            g0, g1 = images[0] * HEADS, (images[-1] + 1) * HEADS
            for s in range(PARTS):
                for t in range(PARTS):
                    r0 = (s * PARTS + t) * HC
                    if what == "q":
                        dst = qst[r0:r0 + HC, g0:g1, :]
                        src = q_dram[HC * g0:HC * g1, s, :].rearrange("(g c) n -> c g n", c=HC)
                    else:
                        dst = kst[r0:r0 + HC, g0:g1, 0:KEYS]
                        src = k_dram[HC * g0:HC * g1, t, :].rearrange("(g c) n -> c g n", c=HC)
                    queue.dma_start(dst, src).then_inc(signal, 16)

        NG = PARTS * PARTS * 16

        def mode_part(engine, g, part):
            rows = slice(32 * g, 32 * g + 32)
            dst = xm[rows, :, 8 * g + 4 * part:8 * g + 4 * part + 4]
            v = tmp3[rows, 4, :].rearrange("p (n b) -> p n b", b=B)
            u = tmp3[rows, 3, :].rearrange("p (n b) -> p n b", b=B)
            return engine.tensor_tensor(dst, v, u, ALU.subtract if part else ALU.add)

        GN_STEPS = 3 + 3 + 6
        Q_RESID = 3 * GN_STEPS + 1
        K_RESID = Q_RESID + 1

        @block.sync
        def _(sp):
            sp.dma_start(xa[:], x).then_inc(x_loaded, 16)
            sp.dma_start(cst[:, 0:N_FIRST], consts[:, 0:N_FIRST]).then_inc(first_loaded, 16)
            for t in range(3):
                for slot in range(4):
                    if not by_pool(t, slot):
                        copy_slot(sp, t, slot, tile_hw[t])
                if t == 0:
                    sp.dma_start(cst[:, N_FIRST:N_CONST], consts[:, N_FIRST:N_CONST]).then_inc(consts_loaded, 16)
            for layer in (1, 2):
                sp.wait_ge(padded, layer + 1)
                if layer == 1:
                    sp.wait_ge(l0_done, 1)
                for r in (0, 1):
                    replicate(sp, layer, r, rep_hw[layer - 1])
            sp.wait_ge(part_dve, 1)
            sp.dma_start(q_dram, qkparts[:, 0]).then_inc(qd_written, 16)
            sp.wait_ge(part_dve, 2)
            sp.dma_start(k_dram, qkparts[:, 1, :, 0:KEYS]).then_inc(kd_written, 16)
            sp.wait_ge(k_filled, 2)
            sp.wait_ge(qd_written, 16)
            gather_parts(sp, "q", [0], q_in[0])
            sp.wait_ge(kd_written, 16)
            gather_parts(sp, "k", [0], k_in[0])
            gather_parts(sp, "k", [1, 2, 3], k_in[1])
            gather_parts(sp, "q", [1, 2, 3], q_in[1])
            for b in range(B):
                sp.wait_ge(mt_copied, b + 1)
                sp.dma_start(m_dram[b], mt_sb[:]).then_inc(md_written, 16)
                sp.wait_ge(md_written, 16 * (b + 1))
                if b > 0:
                    sp.wait_ge(m_in, 16 * b)
                sp.dma_start(qst[PAIR_ROWS:S_ROWS, b * HEADS:(b + 1) * HEADS, :],
                             m_dram[b].rearrange("(s h a) n -> s h (a n)", s=PARTS, h=HEADS)
                             ).then_inc(m_in, 16)
                if b == 0:
                    sp.wait_ge(v_done, 1)
                    sp.dma_start(wm, wmodes).then_inc(wm_loaded, 16)
            sp.wait_ge(res_ready, 1)
            sp.dma_start(out, xb[:]).then_inc(stored, 16)
            sp.wait_ge(stored, 16)

        @block.gpsimd
        def _(pool):
            nc.gpsimd.memset(xp[:], 0.0).then_inc(xp_zeroed, 1)
            for t in range(3):
                for slot in range(4):
                    if by_pool(t, slot):
                        copy_slot(pool, t, slot, tile_sw[t])
            nc.gpsimd.memset(vt[:], 0.0).then_inc(vt_zeroed, 1)
            nc.gpsimd.memset(vrest[:], 0.0).then_inc(vt_zeroed, 1)
            for layer in (1, 2):
                pool.wait_ge(padded, layer + 1)
                if layer == 1:
                    pool.wait_ge(l0_done, 1)
                replicate(pool, layer, 2, rep_sw[layer - 1])
                if layer == 1:
                    pool.wait_ge(vt_zeroed, 2)
                    nc.gpsimd.memset(kst[64:S_ROWS, :, 0:KEYS], 1.0).then_inc(k_filled, 1)
                    pool.wait_ge(k_filled, 1)
                    nc.gpsimd.memset(kst[0:S_ROWS, :, KEYS:KPAD], 0.0).then_inc(k_filled, 1)
            pool.wait_ge(vt_ready, 1)
            pool.wait_ge(vt_zeroed, 2)
            nc.gpsimd.memset(vt[:, :, :, HC:HC + 1], 1.0).then_inc(vt_zeroed, 1)
            for h in range(HEADS):
                pool.wait_ge(vt_zeroed, 3 + h)
                nc.gpsimd.memset(vrest[32 * h:32 * h + KREST, :, 32 * h + HC:32 * h + HC + 1], 1.0
                                 ).then_inc(vt_zeroed, 1)
            for n in range(2 * B):
                pool.wait_ge(o_read, 2 * (n + 1))
                if n >= 2:
                    pool.wait_ge(attn_ready, n - 1)
                nc.gpsimd.tensor_tensor(on[:, n % 2, :].rearrange("p (a c) -> p a c", c=32),
                                        ot[:, n % 2, :].rearrange("p (a c) -> p a c", c=32),
                                        rden[:, n % 2, :, None].to_broadcast([P, 16, 32]),
                                        ALU.mult).then_inc(o_scaled, 1)
            pool.wait_ge(scored, 2 * B * EXP_UNITS)
            nc.gpsimd.memset(arena_a[:, 0:8192], 0.0).then_inc(xm_zeroed, 1)
            pool.wait_ge(tu_ready, 8)
            pool.wait_ge(xm_zeroed, 1)
            for g in range(4):
                if g:
                    pool.wait_ge(xm_pool, g)
                mode_part(nc.gpsimd, g, 1).then_inc(xm_pool, 1)

        @block.scalar
        def _(act):
            act.wait_ge(consts_loaded, 16)
            act.wait_ge(l1s_done, 1)
            nc.scalar.activation(l1s[:], ps[0:96, 7, 0:96], ACT.Copy).then_inc(l1s_ready, 1)
            act.wait_ge(xin_done, 1)
            act.wait_ge(rep_hw[0], 2 * B * 16)
            act.wait_ge(rep_sw[0], B * 16)
            nc.scalar.activation(interior(xp), banks(4).rearrange("p (y x) -> p y x", x=W), ACT.Identity,
                                 bias=c_("bin")).then_inc(padded, 1)
            act.wait_ge(q_done, 1)
            nc.scalar.activation(qkparts[:, 0, 0, :], banks(0), ACT.Copy).then_inc(part_act, 1)
            act.wait_ge(dve_step, Q_RESID)
            nc.scalar.activation(qkparts[:, 0, 1, :], resid[:, 0, :], ACT.Copy).then_inc(part_act, 1)
            act.wait_ge(k_done, 1)
            nc.scalar.activation(qkparts[:, 1, 0, 0:KEYS].rearrange("p (a n) -> p a n", a=2),
                                 ps[:, 2:4, 0:KHALF], ACT.Copy).then_inc(part_act, 1)
            act.wait_ge(dve_step, K_RESID)
            nc.scalar.activation(qkparts[:, 1, 1, 0:KEYS], resid[:, 1, 0:KEYS], ACT.Copy).then_inc(part_act, 1)
            act.wait_ge(v_done, 1)
            nc.scalar.activation(vs[:].rearrange("p (a n) -> p a n", a=2), ps[:, 6:8, 0:KHALF],
                                 ACT.Copy).then_inc(vs_ready, 1)
            for n in range(2 * B * EXP_UNITS):
                half, i = divmod(n, EXP_UNITS)
                act.wait_ge(scored, n + 1)
                if n >= PRING:
                    old_half, old = divmod(n - PRING, EXP_UNITS)
                    act.wait_ge(pv_done, old_half * (DT + 1) + old // HEADS + 1)
                nc.scalar.activation(probs[:, n % PRING, :], ps[:, n % 4, :], ACT.Exp).then_inc(expd, 1)
            act.wait_ge(gb_ready, 1)
            for i in range(3):
                act.wait_ge(gate_done, i + 1)
                nc.scalar.activation(tmp3[:, i, :], banks(2 * i), ACT.Tanh, bias=gb[:, i:i + 1],
                                     scale=1.0 if i == 1 else 0.5).then_inc(gate_act, 1)
            act.wait_ge(cell_ready, 1)
            nc.scalar.activation(tmp3[:, 4, :], tmp3[:, 3, :], ACT.Tanh, scale=0.5).then_inc(cell_act, 1)

        @block.vector
        def _(dve):
            chain = [0]

            def link(ins):
                chain[0] += 1
                ins.then_inc(dve_step, 1)
                dve.wait_ge(dve_step, chain[0])

            def norm(src, dst):
                link(nc.vector.bn_stats(stats[:, 0:6], src[:, 0:HALF]))
                link(nc.vector.bn_stats(stats[:, 6:12], src[:, HALF:HW]))
                link(nc.vector.bn_aggr(small[:, 0:2], stats[:, :].rearrange("p (a b) -> p a b", b=6)))
                mean, var, v, y, t, nh = (small[:, i:i + 1] for i in range(6))
                link(nc.vector.tensor_scalar(v, var, EPS, None, ALU.add))
                link(nc.vector.tensor_scalar(y.bitcast(I32), v.bitcast(I32), -0.5, float(0x5F3759DF),
                                             ALU.mult, ALU.add))
                link(nc.vector.tensor_scalar(nh, v, -0.5, None, ALU.mult))
                for _ in range(3):
                    link(nc.vector.scalar_tensor_tensor(t, y, nh, y, ALU.mult, ALU.mult))
                    link(nc.vector.scalar_tensor_tensor(y, t, 1.5, y, ALU.add, ALU.mult))
                return nc.vector.tensor_scalar(dst, src3(src, dst), mean, y, ALU.subtract, ALU.mult)

            def src3(src, dst):
                return src.rearrange("p (y x) -> p y x", x=W) if len(dst.shape) == 3 else src

            dve.wait_ge(x_loaded, 16)
            dve.wait_ge(xp_zeroed, 1)
            norm(xa[:], interior(xp)).then_inc(padded, 1)
            dve.wait_ge(padded, 1)
            for m, (dy, dx) in enumerate(MAPS):
                at = dy * WP + dx
                nc.vector.scalar_tensor_tensor(maps[:, m, :], xp[:, 0:MAPW], VOLTERRA_SCALE,
                                               xp[:, at:at + MAPW], ALU.mult, ALU.mult).then_inc(map_ready, 1)
            dve.wait_ge(l0_done, 1)
            dve.wait_ge(first_loaded, 16)
            l0t = stack[:, 2, 0, 0:HW]
            nc.vector.transpose(l0t.rearrange("p (j o) -> p j o", o=32),
                                banks(0).rearrange("p (i j) -> p j i", j=32)).then_inc(l0_read, 1)
            dve.wait_ge(l0_read, 1)
            nc.vector.scalar_tensor_tensor(xb[:], l0t, c_("l0bias"), xa[:], ALU.add, ALU.add).then_inc(l0_read, 1)
            dve.wait_ge(l0_read, 2)
            dve.wait_ge(tile_hw[0], (4 - pool_tiles[0]) * B * 16)
            norm(xb[:], interior(xp)).then_inc(padded, 1)
            dve.wait_ge(consts_loaded, 16)
            dve.wait_ge(l1_done, 1)
            nc.vector.scalar_tensor_tensor(xc[:], banks(2), c_("l1bias"), xb[:], ALU.add, ALU.add
                                           ).then_inc(l1_read, 1)
            dve.wait_ge(l1_read, 1)
            norm(xc[:], xa[:]).then_inc(xn2_ready, 1)
            nc.vector.tensor_scalar(xb[:], xc[:], c_("bout"), None, ALU.add).then_inc(l1_read, 1)
            nc.vector.tensor_copy(ident_b[:], c_("ident")).then_inc(l1_read, 1)
            dve.wait_ge(padded, 3)
            rows = xp[:, WP:WP + 32 * WP].rearrange("p (y x) -> p y x", x=WP)
            for v in range(3):
                nc.vector.tensor_reduce(wsum[:, v, :], rows[:, :, 1 + v:1 + v + KH], AX.X, ALU.add
                                        ).then_inc(win_ready, 1)
            dve.wait_ge(win_ready, 3)
            for u in range(3):
                nc.vector.tensor_reduce(win9[:, 3 * u:3 * u + 3], wsum[:, :, u:u + KH], AX.X, ALU.add
                                        ).then_inc(win_ready, 1)
            dve.wait_ge(part_act, 1)
            link(nc.vector.tensor_tensor(resid[:, 0, :], banks(0), qkparts[:, 0, 0, :], ALU.subtract))
            dve.wait_ge(part_act, 2)
            nc.vector.tensor_tensor(qkparts[:, 0, 2, :], resid[:, 0, :], qkparts[:, 0, 1, :], ALU.subtract
                                    ).then_inc(part_dve, 1)
            dve.wait_ge(part_act, 3)
            link(nc.vector.tensor_tensor(resid[:, 1, 0:KEYS].rearrange("p (a n) -> p a n", a=2),
                                         ps[:, 2:4, 0:KHALF],
                                         qkparts[:, 1, 0, 0:KEYS].rearrange("p (a n) -> p a n", a=2),
                                         ALU.subtract))
            assert chain[0] == K_RESID
            dve.wait_ge(part_act, 4)
            nc.vector.tensor_tensor(qkparts[:, 1, 2, 0:KEYS], resid[:, 1, 0:KEYS], qkparts[:, 1, 1, 0:KEYS],
                                    ALU.subtract).then_inc(part_dve, 1)
            dve.wait_ge(a2_done, 1)
            nc.vector.tensor_scalar(a2[:], ps[:, 5, 0:1], 1.0 / KEYS, None, ALU.mult).then_inc(a2_ready, 1)
            dve.wait_ge(gb_done, 1)
            link(nc.vector.tensor_tensor(gb[:], ps[:, 5, 8:11], c_("gbias"), ALU.add))
            for i in (0, 2):
                last = nc.vector.tensor_scalar(gb[:, i:i + 1], gb[:, i:i + 1], 0.5, None, ALU.mult)
                last.then_inc(gb_ready, 1)
            dve.wait_ge(vt_zeroed, 2)
            dve.wait_ge(vt_done, 1)
            nc.vector.tensor_copy(vt[:, 0:4, :, 0:HC],
                                  ps[:, 4, :].rearrange("p (t g c) -> p t g c", t=4, c=HC)).then_inc(vt_ready, 1)
            dve.wait_ge(vt_done, 2)
            nc.vector.tensor_copy(vt[:, 4:DT, :, 0:HC],
                                  ps[:, 5, 0:(DT - 4) * P].rearrange("p (t g c) -> p t g c", t=DT - 4, c=HC)
                                  ).then_inc(vt_ready, 1)
            for h in range(HEADS):
                r = slice(32 * h, 32 * h + KREST)
                nc.vector.tensor_copy(vrest[r, :, 32 * h:32 * h + HC],
                                      ps[r, 5, 3 * P:4 * P].rearrange("p (b h c) -> p b h c", h=HEADS, c=HC)[:, :, h, :]
                                      ).then_inc(vt_ready, 1)

            def read_output(n):
                dve.wait_ge(pv_done, (n + 1) * (DT + 1))
                if n >= 2:
                    dve.wait_ge(o_scaled, n - 1)
                nc.vector.transpose(ot[:, n % 2, :], ps[:, 6 + n % 2, :]).then_inc(o_read, 1)
                dve.wait_ge(o_read, 2 * n + 1)
                nc.vector.reciprocal(rden[:, n % 2, :, None],
                                     ot[:, n % 2, :].rearrange("p (a c) -> p a c", c=32)[:, :, HC:HC + 1]
                                     ).then_inc(o_read, 1)

            def write_output(n):
                dve.wait_ge(o_scaled, n + 1)
                b, half = divmod(n, 2)
                nc.vector.transpose(attn[:, b, half * HALF:(half + 1) * HALF], on[:, n % 2, :]
                                    ).then_inc(attn_ready, 1)

            def split_max(b):
                dve.wait_ge(max_read, MU * b + MAX_UNITS)
                link(nc.vector.tensor_reduce(negm[:, 0, :], mx[:].rearrange("p (a e) -> p a e", e=2), AX.X,
                                             ALU.max, negate=True))
                if b > 0:
                    dve.wait_ge(max_scored, MU * b)
                link(nc.vector.tensor_copy(mparts[:, 0, :], negm[:, 0, :]))
                link(nc.vector.tensor_tensor(negm[:, 1, :], negm[:, 0, :], mparts[:, 0, :], ALU.subtract))
                link(nc.vector.tensor_copy(mparts[:, 1, :], negm[:, 1, :]))
                nc.vector.tensor_tensor(mparts[:, 2, :], negm[:, 1, :], mparts[:, 1, :], ALU.subtract
                                        ).then_inc(m_split, 1)
                n = MU * b + MAX_UNITS
                dve.wait_ge(max_scored, n + 1)
                if b > 0:
                    dve.wait_ge(md_written, 16 * b)
                nc.vector.tensor_copy(mt_sb[:], ps[0:PARTS * MAX_UNITS // 2, 4 + n % 2, 0:P // 2].bitcast(BF16)
                                      ).then_inc(mt_copied, 1)

            for b in range(B):
                for u in range(MAX_UNITS):
                    n = MU * b + u
                    dve.wait_ge(max_scored, n + 1)
                    nc.vector.tensor_reduce(mx[:, u:u + 1], ps[:, 4 + n % 2, 0:KHALF], AX.X, ALU.max
                                            ).then_inc(max_read, 1)
                    if b > 1 and u == 4:
                        read_output(2 * b - 3)
                    if b > 1 and u == 8:
                        write_output(2 * b - 3)
                    if b > 0 and u == 44:
                        read_output(2 * b - 2)
                    if b > 0 and u == 50:
                        write_output(2 * b - 2)
                split_max(b)
                dve.wait_ge(mt_copied, b + 1)
                nc.vector.tensor_copy(small[:, 8:9], small[:, 0:1]).then_inc(max_read, 1)
            for n in range(2 * B - 3, 2 * B):
                read_output(n)
                write_output(n)
            dve.wait_ge(gate_act, 2)
            nc.vector.scalar_tensor_tensor(tmp3[:, 3, :], tmp3[:, 0, :], 1.0, tmp3[:, 1, :], ALU.add, ALU.mult
                                           ).then_inc(cell_ready, 1)
            dve.wait_ge(gate_act, 3)
            dve.wait_ge(cell_act, 1)
            nc.vector.scalar_tensor_tensor(tmp3[:, 5, :], tmp3[:, 2, :], 1.0, tmp3[:, 4, :], ALU.add, ALU.mult
                                           ).then_inc(h_ready, 1)
            dve.wait_ge(wout_done, 1)
            dve.wait_ge(l1_read, 3)
            nc.vector.scalar_tensor_tensor(xc[:], banks(6), 0.5, xb[:], ALU.mult, ALU.add).then_inc(x3_ready, 1)
            dve.wait_ge(x3_ready, 1)
            link(norm(xc[:], xa[:]))
            nc.vector.transpose(tmp3[:, 0, :].rearrange("p (w c) -> p w c", c=C),
                                xa[:, :].rearrange("p (h w) -> p w h", w=W)).then_inc(t1_ready, 1)
            for i in range(2):
                dve.wait_ge(rows_done, i + 1)
                nc.vector.transpose(tmp3[:, 1 + i, :].rearrange("p (c k) -> p c k", k=MODES),
                                    banks(2 * i).rearrange("p (w c) -> p c w", c=C)).then_inc(t2_ready, 1)
            for i in range(2):
                dve.wait_ge(cols_done, i + 1)
                src = banks(4 + 2 * i).rearrange("p (b c k) -> p b k c", b=B, c=C)
                dst = tmp3[:, 3 + i, :].rearrange("p (k l b) -> p b k l", b=B, l=MODES)
                for b in range(B):
                    last = nc.vector.transpose(dst[:, b], src[:, b])
                    last.then_inc(tu_ready, 1)
            dve.wait_ge(tu_ready, 8)
            dve.wait_ge(xm_zeroed, 1)
            for g in range(4):
                mode_part(nc.vector, g, 0).then_inc(xm_dve, 1)
            dve.wait_ge(mix_done, 1)
            for k2 in range(2):
                nc.vector.transpose(y1[:, k2 * HW:(k2 + 1) * HW].rearrange("p (o m) -> p o m", m=32),
                                    banks(2 * k2).rearrange("p (l o) -> p o l", o=C)).then_inc(y1_ready, 1)
            for s in range(2):
                dve.wait_ge(inv_l_done, s + 1)
                nc.vector.transpose(z1[:, s * HW:(s + 1) * HW], banks(4 + 2 * s)).then_inc(z1_ready, 1)
            dve.wait_ge(inv_k_done, 1)
            link(nc.vector.transpose(tmp3[:, 0, :].rearrange("p (k l) -> p l k", l=W),
                                     banks(0).rearrange("p (o l) -> p l o", l=W)))
            nc.vector.scalar_tensor_tensor(xb[:], tmp3[:, 0, :], 0.5 / HW, xc[:], ALU.mult, ALU.add
                                           ).then_inc(res_ready, 1)

        @block.tensor
        def _(pe):
            mm = nc.tensor.matmul
            l0w = c_("l0w").rearrange("p (s o) -> p s o", o=32)
            single = c_("l0single").rearrange("p (s o) -> p s o", o=P)
            pe.wait_ge(first_loaded, 16)
            for m, (_, (py, px)) in enumerate(SINGLES):
                pe.wait_ge(map_ready, m + 1)
                for e in range(2):
                    mm(ps[:, e, :].rearrange("p (y x) -> p y x", x=W), single[:, m, :],
                       window(maps[:, m, :], py, px, 16 * e, 16, W), start=(m == 0), stop=False,
                       skip_group_check=True)
            for s, (t, (py, px)) in enumerate(SLOTS):
                if s == 0 or SLOTS[s - 1][0] != t:
                    pe.wait_ge(tile_hw[t], (4 - pool_tiles[t]) * B * 16)
                    pe.wait_ge(tile_sw[t], pool_tiles[t] * B * 16)
                for e in range(2):
                    for b in range(B):
                        last = mm(ps[32 * b:32 * b + 32, e, :].rearrange("p (y x) -> p y x", x=W), l0w[:, s, :],
                                  window(stack[:, t, b, :], py, px, 16 * e, 16, W), start=False,
                                  stop=(s == len(SLOTS) - 1), skip_group_check=True)
            last.then_inc(l0_done, 1)

            def conv(bank, weights, tile, rows, cols, first, signal):
                ny = rows // 2
                for e in range(2):
                    for px in range(3):
                        for b in range(B):
                            last = mm(ps[32 * b:32 * b + 32, bank + e, 0:ny * cols].rearrange("p (y x) -> p y x", x=cols),
                                      weights[:, px, :],
                                      window(stack[0:96, tile, b, :], first, first + px, ny * e, ny, cols),
                                      start=(px == 0), stop=(px == 2))
                last.then_inc(signal, 1)

            pe.wait_ge(consts_loaded, 16)
            mm(ps[0:96, 7, 0:96], c_("ones", 0, 96)[:, 0:96], c_("l1w", 0, 96), start=True, stop=True
               ).then_inc(l1s_done, 1)
            pe.wait_ge(l1s_ready, 1)
            pe.wait_ge(rep_hw[0], 2 * B * 16)
            pe.wait_ge(rep_sw[0], B * 16)
            conv(2, l1s[:].rearrange("p (s o) -> p s o", o=32), 0, H, W, 0, l1_done)

            pe.wait_ge(xn2_ready, 1)
            for e in range(2):
                last = mm(ps[:, 4 + e, :], c_("win"), xa[:, e * HALF:(e + 1) * HALF], start=True, stop=True)
            last.then_inc(xin_done, 1)
            pe.wait_ge(l0_read, 1)
            pe.wait_ge(l1_read, 1)
            pe.wait_ge(rep_hw[1], 2 * B * 16)
            pe.wait_ge(rep_sw[1], B * 16)
            qkv = c_("qkv", 0, 96).rearrange("p (a s o) -> p a s o", a=3, o=32)
            conv(0, qkv[:, 0], 1, H, W, 0, q_done)
            conv(2, qkv[:, 1], 1, KH, KH, 1, k_done)
            conv(6, qkv[:, 2], 1, KH, KH, 1, v_done)
            pe.wait_ge(padded, 3)
            pe.wait_ge(win_ready, 6)
            v2w = c_("v2w").rearrange("p (s o) -> p s o", o=32)
            for b in range(B):
                r = slice(32 * b, 32 * b + 32)
                for s in range(9):
                    last = mm(ps[r, 5, 0:1], v2w[r, s, :], win9[r, s:s + 1], start=(s == 0), stop=(s == 8))
            last.then_inc(a2_done, 1)
            pe.wait_ge(a2_ready, 1)
            proj2 = c_("proj2").rearrange("p (s o) -> p s o", o=32)
            for b in range(B):
                r = slice(32 * b, 32 * b + 32)
                for i in range(3):
                    last = mm(ps[r, 5, 8 + i:9 + i], proj2[r, i, :], a2[r, :], start=True, stop=True)
            last.then_inc(gb_done, 1)
            pe.wait_ge(vs_ready, 1)
            pe.wait_ge(gb_ready, 2)
            for t in range(DT):
                last = nc.tensor.transpose(ps[:, 4 + t // 4, (t % 4) * P:(t % 4 + 1) * P],
                                           vs[:, t * P:(t + 1) * P], c_("ident"))
                if t == 3:
                    last.then_inc(vt_done, 1)
            for h in range(HEADS):
                last = mm(ps[32 * h:32 * h + KREST, 5, 3 * P:4 * P], vs[:, DT * P:KEYS], c_("ident"),
                          start=True, stop=True)
            last.then_inc(vt_done, 1)
            pe.wait_ge(vt_ready, 2 + HEADS)

            def max_unit(b, u):
                n = MU * b + u
                if n >= 2:
                    pe.wait_ge(max_read, n - 1)
                bank = 4 + n % 2
                if u == MAX_UNITS:
                    pe.wait_ge(m_split, b + 1)
                    nc.tensor.transpose(ps[0:PARTS * MAX_UNITS // 2, bank, 0:P // 2].bitcast(BF16),
                                        mparts[:].rearrange("p s n -> p (s n)"), ident_b[:]).then_inc(max_scored, 1)
                    return
                h, rest = divmod(u, QT_TILES * 2)
                qt, e = divmod(rest, 2)
                g = b * HEADS + h
                mm(ps[:, bank, 0:KHALF], qst[0:PAIR_ROWS, g, qt * P:(qt + 1) * P],
                   kst[0:PAIR_ROWS, g, e * KHALF:(e + 1) * KHALF], start=True, stop=True).then_inc(max_scored, 1)

            def score_tile(n):
                half, i = divmod(n, EXP_UNITS)
                b, e = divmod(half, 2)
                if n >= 4:
                    pe.wait_ge(expd, n - 3)
                queries = slice(e * HALF, (e + 1) * HALF)
                if i < HEADS * DT:
                    t, h = divmod(i, HEADS)
                    g = b * HEADS + h
                    mm(ps[:, n % 4, :], kst[0:S_ROWS, g, t * P:(t + 1) * P], qst[0:S_ROWS, g, queries],
                       start=True, stop=True).then_inc(scored, 1)
                else:
                    for h in range(HEADS):
                        g = b * HEADS + h
                        last = mm(ps[32 * h:32 * h + 32, n % 4, :], kst[0:S_ROWS, g, DT * P:KPAD],
                                  qst[0:S_ROWS, g, queries], start=True, stop=True)
                    last.then_inc(scored, 1)

            def values(half, t):
                b = half // 2
                bank = 6 + half % 2
                n0 = half * EXP_UNITS + t * HEADS
                if t == 0 and half >= 2:
                    pe.wait_ge(o_read, 2 * (half - 1))
                if t < DT:
                    pe.wait_ge(expd, n0 + HEADS)
                    for h in range(HEADS):
                        last = mm(ps[32 * h:32 * h + 32, bank, :], vt[:, t, b * HEADS + h, :],
                                  probs[:, (n0 + h) % PRING, :], start=(t == 0), stop=False,
                                  skip_group_check=True)
                    last.then_inc(pv_done, 1)
                else:
                    pe.wait_ge(expd, n0 + 1)
                    mm(ps[:, bank, :], vrest[:, b, :], probs[:, n0 % PRING, :], start=False, stop=True,
                       skip_group_check=True).then_inc(pv_done, 1)

            pe.wait_ge(vt_zeroed, 3 + HEADS)
            pe.wait_ge(l1_read, 3)
            pe.wait_ge(q_in[0], NG)
            pe.wait_ge(k_in[0], NG)
            for u in range(MU):
                max_unit(0, u)
            for b in range(B):
                todo = list(range(MU)) if b + 1 < B else []
                steps = [(2 * b + e, t) for e in range(2) for t in range(DT + 1)]
                if b == 0:
                    pe.wait_ge(k_in[1], NG)
                    pe.wait_ge(q_in[1], NG)
                pe.wait_ge(m_in, 16 * (b + 1))
                prev = None
                for half, t in steps:
                    n0 = half * EXP_UNITS + t * HEADS
                    for h in range(HEADS if t < DT else 1):
                        score_tile(n0 + h)
                        if todo:
                            max_unit(b + 1, todo.pop(0))
                    if prev:
                        values(*prev)
                    if todo and t < DT:
                        max_unit(b + 1, todo.pop(0))
                    prev = (half, t)
                values(*prev)
                for u in todo:
                    max_unit(b + 1, u)

            proj = c_("proj").rearrange("p (s o) -> p s o", o=32)
            pe.wait_ge(expd, 2 * B * EXP_UNITS)
            pe.wait_ge(attn_ready, 2 * B)
            for i in range(3):
                for e in range(2):
                    for b in range(B):
                        last = mm(ps[32 * b:32 * b + 32, 2 * i + e, :], proj[:, i, :],
                                  attn[:, b, e * HALF:(e + 1) * HALF], start=True, stop=True)
                last.then_inc(gate_done, 1)
            pe.wait_ge(h_ready, 1)
            for e in range(2):
                last = mm(ps[:, 6 + e, :], c_("wout"), tmp3[:, 5, e * HALF:(e + 1) * HALF], start=True, stop=True)
            last.then_inc(wout_done, 1)

            pe.wait_ge(t1_ready, 1)
            for i, m in enumerate(("mt", "mrt")):
                for e in range(2):
                    last = mm(ps[:, 2 * i + e, :], c_(m), tmp3[:, 0, e * HALF:(e + 1) * HALF], start=True, stop=True)
                last.then_inc(rows_done, 1)
            pe.wait_ge(x3_ready, 1)
            for i, m in enumerate(("mt", "mrt")):
                pe.wait_ge(t2_ready, i + 1)
                src = tmp3[:, 1 + i, :].rearrange("p (c k) -> p c k", k=MODES)
                for b in range(B):
                    for g in range(4):
                        dst = ps[32 * g:32 * g + 32, 4 + 2 * i + b // 2, (b % 2) * 256:(b % 2 + 1) * 256]
                        last = mm(dst.rearrange("p (c k) -> p c k", k=KG), c_(m)[:, 32 * b:32 * b + 32],
                                  src[:, :, KG * g:KG * (g + 1)], start=True, stop=True)
                last.then_inc(cols_done, 1)
            pe.wait_ge(wm_loaded, 16)
            pe.wait_ge(xm_dve, 4)
            pe.wait_ge(xm_pool, 4)
            wv = wm.rearrange("p (n o) -> p n o", o=C)
            for k2 in range(2):
                for l in range(MODES):
                    for j in range(4):
                        n = (2 * j + k2) * MODES + l
                        last = mm(banks(2 * k2)[32 * j:32 * j + 32, l * C:(l + 1) * C], xm[:, n, :], wv[:, n, :],
                                  start=True, stop=True)
            last.then_inc(mix_done, 1)
            pe.wait_ge(y1_ready, 2)
            yv = y1.rearrange("p (k o g s b) -> p s b o g k", k=2, o=C, g=4, s=2)
            pe.wait_ge(tu_ready, 8)
            for s, m in enumerate(("mt", "mnt")):
                for oh in range(2):
                    zv = ps[:, 4 + 2 * s + oh, :].rearrange("p (o g j k) -> p j o g k", g=4, j=4, k=2)
                    for j in range(4):
                        for b in range(B):
                            last = mm(zv[32 * b:32 * b + 32, j], c_(m)[:, 32 * j:32 * j + 32],
                                      yv[:, s, b, oh * 16:(oh + 1) * 16], start=(j == 0), stop=True,
                                      skip_group_check=True)
                last.then_inc(inv_l_done, 1)
            for s, m in enumerate(("mt", "mnt")):
                pe.wait_ge(z1_ready, s + 1)
                for e in range(2):
                    last = mm(ps[:, e, :], c_(m), z1[:, s * HW + e * HALF:s * HW + (e + 1) * HALF],
                              start=(s == 0), stop=(s == 1))
            last.then_inc(inv_k_done, 1)



def transform_matrix(n):
    if n == 1:
        return np.ones((1, 1), np.float32)
    m = transform_matrix(n // 2)
    k = np.arange(n // 2)
    cas = (np.cos(2 * np.pi * k / n) + np.sin(2 * np.pi * k / n)).astype(np.float32)[:, None]
    even = np.zeros((n // 2, n), np.float32)
    even[:, 0::2] = m
    odd = np.zeros((n // 2, n), np.float32)
    odd[:, 1::2] = m
    return np.concatenate([even + cas * odd, even - cas * odd], axis=0)


def blocks(m):
    out = np.zeros((P, P), np.float32)
    for b in range(B):
        out[32 * b:32 * b + 32, 32 * b:32 * b + 32] = m
    return out


def layout_consts(i):
    c = np.zeros((P, N_CONST), np.float32)

    def put(name, value, rows=P):
        at, n = CONSTS[name]
        c[0:rows, at:at + n] = np.asarray(value).reshape(rows, n)

    w1 = np.asarray(i["L0_conv_W1"]).reshape(C, 9, 32)
    w2 = np.asarray(i["L0_conv_W2"]).reshape(C, 9, 9, 32)
    l0 = np.zeros((4, C, len(SLOTS), 32), np.float32)
    for s, (t, (py, px)) in enumerate(SLOTS):
        for slot, (d, pre) in enumerate(TILES[t]):
            pair = tap_pair(d, pre, py, px)
            if pair:
                l0[slot, :, s, :] = w1[:, pair[0]] if d is LINEAR else w2[:, pair[0], pair[1]]
    put("l0w", l0)
    put("l0single", np.stack([blocks(w2[:, py * 3 + px, (py + dy) * 3 + px + dx])
                              for (dy, dx), (py, px) in SINGLES], axis=1))
    put("l0bias", np.tile(np.asarray(i["L0_conv_bias_w"]).reshape(32), B))
    put("l1w", np.asarray(i["L1_conv_weight"])[:, :, ::-1, ::-1].transpose(2, 1, 3, 0), 96)
    put("ones", blocks(np.ones((32, 32), np.float32)))
    put("l1bias", np.tile(np.asarray(i["L1_conv_bias"]), B))
    put("win", blocks(np.asarray(i["L2_conv_W_in"]).T))
    put("bin", np.tile(np.asarray(i["L2_conv_b_in"]), B))
    qkv = np.stack([np.asarray(i["L2_conv_" + n])[0] for n in ("Wq", "Wk", "Wv")])
    put("qkv", qkv.transpose(3, 2, 0, 4, 1), 96)
    put("v2w", np.tile(np.asarray(i["L2_conv_Wv"])[2].reshape(32, C, 9).transpose(1, 2, 0), (B, 1, 1)))
    wproj = np.asarray(i["L2_conv_Wproj"])[list(GATES)]
    proj = np.zeros((HEADS, 32, 3, 32), np.float32)
    proj[:, 0:HC] = wproj[:, 0].reshape(3, 32, HEADS, HC).transpose(2, 3, 0, 1)
    put("proj", proj)
    put("proj2", np.tile(wproj[:, 2].transpose(2, 0, 1), (B, 1, 1)))
    put("gbias", np.tile(np.asarray(i["L2_conv_b_gates"])[list(GATES)].T, (B, 1)))
    put("wout", blocks(np.asarray(i["L2_conv_W_out"]).T))
    put("bout", np.tile(np.asarray(i["L2_conv_b_out"]), B))
    put("ident", np.eye(P, dtype=np.float32))
    m = transform_matrix(MODES)
    neg = -np.arange(MODES) % MODES
    put("mt", blocks(m.T))
    put("mrt", blocks(m[neg].T))
    put("mnt", blocks(m[:, neg].T))
    return c


def kernel(**inputs):
    import concourse.bacc as bacc
    from concourse.bass_utils import run_bass_kernel_spmd

    wmodes = np.asarray(inputs["L3_conv_weights1"])
    wmodes = wmodes.reshape(C, 32, 4, KG, MODES).transpose(2, 0, 3, 4, 1).reshape(P, KG * MODES * 32)
    arrays = {"x": np.ascontiguousarray(np.asarray(inputs["x"]).reshape(P, HW)),
              "consts": layout_consts(inputs), "wmodes": np.ascontiguousarray(wmodes)}
    nc = bacc.Bacc("TRN2", target_bir_lowering=False, num_devices=1)
    args = [nc.dram_tensor(n, a.shape, F32, kind="ExternalInput").ap() for n, a in arrays.items()]
    out = nc.dram_tensor("out", [P, HW], F32, kind="ExternalOutput").ap()
    build(nc, *args, out)
    r = run_bass_kernel_spmd(nc, [arrays], core_ids=[0])
    return r.results[0]["out"].reshape(B, C, H, W)
```

```python
from contextlib import ExitStack

import numpy as np

import concourse.bass as bass
from concourse import mybir

F32 = mybir.dt.float32
BF16 = mybir.dt.bfloat16
I32 = mybir.dt.int32
ACT = mybir.ActivationFunctionType
ALU = mybir.AluOpType
AX = mybir.AxisListType

P = 128
B, C, H, W = 4, 32, 32, 32
HW = H * W
HALF = HW // 2
WP = W + 2
NP = WP * WP
XPW = NP + 76
EPS = 1e-5

LINEAR = None
TILES = [
    ([(LINEAR, (0, 0)), ((0, 0), (0, 0)), ((0, 1), (0, 0)), ((1, 0), (0, 0))],
     [(py, px) for py in range(3) for px in range(3)]),
    ([((1, 1), (0, 0)), ((1, -1), (0, 1)), ((2, 0), (0, 0)), ((0, 2), (0, 0))],
     [(0, 0), (0, 1), (1, 0), (1, 1)]),
    ([((1, 2), (0, 0)), ((1, -2), (0, 2)), ((2, 0), (0, 2)), ((0, 2), (2, 0))], [(0, 0), (1, 0)]),
    ([((2, 1), (0, 0)), ((2, -1), (0, 1)), ((2, 2), (0, 0)), ((2, -2), (0, 2))], [(0, 0), (0, 1)]),
]
SLOTS_PER_TILE = P // C
N_MAPS = SLOTS_PER_TILE * len(TILES)
PLANE = 386
TOP = 18 * WP
CUTS = ((0, TOP), (TOP, NP))


def tap_pair(d, pre, py, px):
    dy, dx = d or (0, 0)
    py, px = py + pre[0], px + pre[1]
    qy, qx = py + dy, px + dx
    if max(py, px) > 2 or not (0 <= qy <= 2 and 0 <= qx <= 2):
        return None
    return py * 3 + px, qy * 3 + qx


SLOTS = [(t, offset) for t, (_, offsets) in enumerate(TILES) for offset in offsets]
N_KEPT = 45
_pairs = [(d is LINEAR, tap_pair(d, pre, *offset)) for maps, offsets in TILES for d, pre in maps
          for offset in offsets if tap_pair(d, pre, *offset)]
assert len(_pairs) == len(set(_pairs)) == 9 + N_KEPT
VOLTERRA_SCALE = float(np.float32(1.0 / np.sqrt(N_KEPT)))

HEADS, HC = 4, 8
G = B * HEADS
KH = H - 2
KEYS = KH * KH
KHALF = KEYS // 2
DT = KEYS // P
KREST = KEYS - DT * P
KPAD = DT * P + 32
KDIFF = KPAD
KW = KPAD + KHALF
PARTS = 3
PAIR_ROWS = PARTS * PARTS * HC
S_ROWS = PAIR_ROWS + PARTS
QT_TILES = HW // P
HALF_TILES = HALF // P
ROWS_OF_MAX = HEADS * HALF_TILES
EXP_UNITS = HEADS * DT + 1
PRING = 8
TWO_ONES = float(np.array([0x3F803F80], np.uint32).view(np.float32)[0])
GATES = (0, 2, 3)
SCORE_RING = (0, 1, 2)
MAX_RING = (3, 4, 5)
O_RING = (6, 7)
GATE_BANKS = (3, 4, 5)
OUT_BANK = 4
MODES = 32
KG = MODES // 4



def attention_plan():
    stream, i = [], 0
    for s in range(2 * B):
        for a in range(ROWS_OF_MAX):
            pair = s < 2 or a % 2 == 0
            for kind in (("diff", "first") if pair else ("first", "second")):
                stream.append(("max", i, s, a, kind))
                i += 1
        stream.append(("split", s))
        stream.append(("turn", i, s))
        i += 1
    for at in [at for at, item in enumerate(stream) if item[0] == "turn"]:
        n = min(MOVED, len(stream) - 1 - at)
        moved = stream[at + 1:at + 1 + n] + [stream[at]]
        numbers = sorted(item[1] for item in moved)
        stream[at:at + 1 + n] = [(item[0], k, *item[2:]) for item, k in zip(moved, numbers)]
    plan = []

    def take(n):
        while n > 0 and stream:
            item = stream.pop(0)
            plan.append(item)
            if item[0] != "split":
                n -= 1

    take(2 * ROWS_OF_MAX + 1 + FIRST_AHEAD)
    due, prev, later, step = 0.0, None, [], 0
    for s in range(2 * B):
        for t in range(DT + 1):
            units = HEADS if t < DT else 1
            due += BLOCKS_PER_STEP * (1.0 if t < DT else 0.6)
            chunks = [("values", *prev, c) for c in range(2)] if prev else []
            taken = 0
            for h in range(units):
                plan.append(("score", s * EXP_UNITS + t * HEADS + h))
                k = int(due * (h + 1) / units + 1e-6)
                take(k - taken)
                taken = max(taken, k)
                if h % 2 == 1 and chunks:
                    plan.append(chunks.pop(0))
            plan.extend(chunks)
            due -= taken
            if prev and prev[1] == DT:
                later += [(step, ("read", prev[0])), (step + 1, ("write", prev[0]))]
                if prev[0] == 2 * B - 2:
                    later += [(step + 1, ("gates", 0)), (step + 2, ("cell", 0)), (step + 3, ("hidden", 0)),
                              (step + 4, ("out", 0))]
            plan += [item for at, item in later if at <= step]
            later = [(at, item) for at, item in later if at > step]
            prev = (s, t)
            step += 1
    plan += [("values", *prev, c) for c in range(2)] + [item for _, item in later]
    plan += [("read", prev[0]), ("write", prev[0])]
    plan += [(name, 1) for name in ("gates", "cell", "hidden", "out")]
    assert not stream
    return plan


MOVED = 4
WIDE_AHEAD = 12
FIRST_AHEAD = 18
BLOCKS_PER_STEP = 4.15
WARM_MAP = 5
W11 = 11
MODE_STAGES = [(k2, lh) for k2 in range(2) for lh in range(2)]
W12 = 9
WARM_L0, W1, W2, W3, W4, W5, W6, W7, W8, W9, W10 = 12, 3, 4, 11, 3, 2, 8, 16, 9, 9, 5
POOL_MODES = 2

CONSTS = {}


def _place(names):
    at = 0
    for name, n in names:
        CONSTS[name] = (at, n)
        at += n
    return at


N_FIRST = _place([("l0w", len(SLOTS) * 32), ("l0bias", 1)])
N_CONST = N_FIRST
for _name, _n in [("l1w", 3 * 32), ("bsel", 32), ("dmask", B), ("l1bias", 1), ("win", P), ("bin", 1), ("qkv", 3 * 3 * 32),
                  ("v2w", 9 * 32), ("proj", 3 * 32), ("proj2", 3 * 32), ("ones", P), ("gbias", 3), ("wout", P),
                  ("bout", 1), ("ident", P), ("mt", P), ("mrt", P), ("mnt", P), ("mt_back", P),
                  ("mnt_back", P)]:
    CONSTS[_name] = (N_CONST, _n)
    N_CONST += _n


def build(nc, x, consts, wmodes, out):
    ctx = ExitStack()
    with ctx:
        def sb(name, shape, dt=F32):
            return ctx.enter_context(nc.sbuf_tensor(name, shape, dt))

        def sem(name):
            return ctx.enter_context(nc.semaphore(name))

        xa = sb("xa", [P, HW])
        xb = sb("xb", [P, HW])
        xc = sb("xc", [P, HW])
        xp = sb("xp", [P, XPW])
        cst = sb("cst", [P, N_CONST])
        stats = sb("stats", [P, 12])
        small = sb("small", [P, 16])
        arena_a = sb("arena_a", [P, 8192 + G * KW // 2])
        arena_b = sb("arena_b", [P, 16384])
        vt = sb("vt", [P, DT, G, 32])
        vrest = sb("vrest", [P, B, P])
        ot = sb("ot", [P, 2, HALF])
        on = sb("on", [P, 2, HALF])
        rden = sb("rden", [P, 2, 16])
        relus = sb("relus", [P, 3, KHALF])
        sums = sb("sums", [P, 2, KHALF], BF16)
        mx = sb("mx", [P, ROWS_OF_MAX, 2])
        negm = sb("negm", [P, 2, ROWS_OF_MAX])
        mparts = sb("mparts", [P, PARTS, ROWS_OF_MAX], BF16)
        mt_sb = sb("mt_sb", [PARTS * ROWS_OF_MAX, P], BF16)
        ident_b = sb("ident_b", [P, P], BF16)
        wsum = sb("wsum", [P, 3, H])
        win9 = sb("win9", [P, 2, 9])
        a2 = sb("a2", [P, 1])
        gb = sb("gb", [P, 3])
        l1s = sb("l1s", [96, 3, P])
        zeros = sb("zeros", [P, 512], BF16)

        def c_(name, r0=0, r1=P):
            at, n = CONSTS[name]
            return cst[r0:r1, at:at + n]

        maps = arena_a[:, 0:N_MAPS * NP].rearrange("p (m n) -> p m n", n=NP)
        q_words = G * HW // 2
        k_words = G * KW // 2
        qst = arena_a[:, 0:q_words].bitcast(BF16).rearrange("p (e g n) -> p e g n", e=2, g=G)
        kst = arena_a[:, q_words:q_words + k_words].bitcast(BF16).rearrange("p (g n) -> p g n", g=G)
        xm = arena_a[:, 0:8192].rearrange("p (n m) -> p n m", m=64)
        tmp3 = arena_a[:, 8192:8192 + 6 * HW].rearrange("p (t n) -> p t n", n=HW)
        stack = arena_b[:, 0:3 * B * NP].rearrange("p (t b n) -> p t b n", t=3, b=B)
        xst = arena_b[:, 0:B * H * WP].rearrange("p (b n) -> p b n", b=B)
        at = B * H * WP
        q_res = arena_b[:, at:at + HW]
        k_res = arena_b[:, at + HW:at + HW + KW]
        at += HW + KW
        k_first = arena_b[:, at:at + KHALF]
        vs = arena_b[:, at + KHALF:at + KHALF + KEYS]
        assert at + KHALF + KEYS <= 8192
        q_parts = arena_b[:, 8192:8192 + PARTS * HW // 2].bitcast(BF16).rearrange("p (s n) -> p s n", s=PARTS)
        at = 8192 + PARTS * HW // 2
        k_parts = arena_b[:, at:at + PARTS * KW // 2].bitcast(BF16).rearrange("p (s n) -> p s n", s=PARTS)
        at += PARTS * KW // 2
        planes = arena_b[:, at:at + 3 * PLANE]
        assert at + 3 * PLANE <= 16384
        probs = arena_b[:, 0:PRING * HALF].rearrange("p (s n) -> p s n", n=HALF)
        attn = arena_b[:, 4096:8192].rearrange("p (b n) -> p b n", b=B)
        wm = arena_b[:, 8192:16384]
        y1 = arena_b[:, 0:4 * HW]
        z1 = arena_b[:, 4 * HW:6 * HW]

        ps = ctx.enter_context(nc.psum_tensor("ps", [P, 8, 512], F32))

        def banks(i, n=2):
            return ps[:, i:i + n, :].rearrange("p a n -> p (a n)")

        q_dram = nc.dram_tensor("q_scratch", [PARTS, 2, HC, G, HALF], BF16, kind="Internal").ap()
        k_dram = nc.dram_tensor("k_scratch", [PARTS, HC, G, KW], BF16, kind="Internal").ap()

        x_loaded = [sem("x_loaded0"), sem("x_loaded1")]
        first_loaded = sem("first_loaded")
        consts_loaded = sem("consts_loaded")
        wm_loaded = sem("wm_loaded")
        dve_step = sem("dve_step")
        padded = sem("padded")
        zeros_ready = sem("zeros_ready")
        xp_zeroed = sem("xp_zeroed")
        act_map = sem("act_map")
        map_ready = sem("map_ready")
        tile0_top = sem("tile0_top")
        tile_in = [sem(f"tile_in{t}") for t in range(len(TILES))]
        l0_done = sem("l0_done")
        l0_read = sem("l0_read")
        l1s_done = sem("l1s_done")
        l1s_ready = sem("l1s_ready")
        planes_done = sem("planes_done")
        planes_ready = sem("planes_ready")
        l1_done = sem("l1_done")
        l1_read = sem("l1_read")
        xst_zeroed = sem("xst_zeroed")
        xin_done = sem("xin_done")
        xin_act = sem("xin_act")
        xin_dve = sem("xin_dve")
        xin_ready = sem("xin_ready")
        k_zeroed = sem("k_zeroed")
        q_done = sem("q_done")
        k_done = sem("k_done")
        v_done = sem("v_done")
        part_act = sem("part_act")
        part_dve = sem("part_dve")
        k_rounded = sem("k_rounded")
        vs_ready = sem("vs_ready")
        vt_done = sem("vt_done")
        vt_ready = sem("vt_ready")
        vt_zeroed = sem("vt_zeroed")
        win_ready = sem("win_ready")
        win_done = sem("win_done")
        win_scaled = sem("win_scaled")
        a2_done = sem("a2_done")
        a2_ready = sem("a2_ready")
        gb_done = sem("gb_done")
        gb_ready = sem("gb_ready")
        qd_written = [sem("qd_written0"), sem("qd_written1")]
        kd_written = sem("kd_written")
        q_filled = sem("q_filled")
        k_filled = sem("k_filled")
        k_padded = sem("k_padded")
        tile0_used = sem("tile0_used")
        q_in = [sem(f"q_in{i}") for i in range(3)]
        k_in = [sem(f"k_in{i}") for i in range(3)]
        max_scored = sem("max_scored")
        max_read = sem("max_read")
        max_relu = sem("max_relu")
        m_split = sem("m_split")
        m_in = sem("m_in")
        scored = sem("scored")
        expd = sem("expd")
        pv_done = sem("pv_done")
        o_read = sem("o_read")
        o_summed = sem("o_summed")
        o_scaled = sem("o_scaled")
        attn_ready = sem("attn_ready")
        gate_done = sem("gate_done")
        gate_act = sem("gate_act")
        cell_ready = sem("cell_ready")
        cell_act = sem("cell_act")
        h_ready = sem("h_ready")
        wout_done = sem("wout_done")
        x3_ready = sem("x3_ready")
        xm_zeroed = sem("xm_zeroed")
        t1_ready = sem("t1_ready")
        rows_done = sem("rows_done")
        t2_ready = sem("t2_ready")
        cols_done = sem("cols_done")
        tu_ready = sem("tu_ready")
        xm_dve = sem("xm_dve")
        xm_pool = sem("xm_pool")
        mix_done = sem("mix_done")
        y1_ready = sem("y1_ready")
        inv_l_done = sem("inv_l_done")
        z1_ready = sem("z1_ready")
        inv_k_done = sem("inv_k_done")
        res_ready = sem("res_ready")
        stored = sem("stored")

        block = ctx.enter_context(nc.Block())

        def interior(ap):
            return ap[:, WP + 1:WP + 1 + 32 * WP].rearrange("p (y x) -> p y x", x=WP)[:, :, 0:W]

        def window(image, py, px, y0, ny, nx):
            rows = image[:, (y0 + py) * WP:(y0 + py + ny) * WP].rearrange("p (y x) -> p y x", x=WP)
            return rows[:, :, px:px + nx]

        plan = attention_plan()
        prologue = 2 * ROWS_OF_MAX + WIDE_AHEAD

        def block_bank(i):
            ring = SCORE_RING + MAX_RING if i < prologue else MAX_RING
            return ring[i % len(ring)]

        def block_before(i, bank):
            return max((j for j in range(max(0, i - 14), i) if block_bank(j) == bank), default=None)

        blocks_read = {}
        diffs = []
        split_after = {}
        vector_reads = 0
        for item in plan:
            if item[0] == "split":
                split_after[item[1]] = vector_reads
            elif item[0] == "turn" or (item[0] == "max" and item[4] != "diff"):
                vector_reads += 1
                blocks_read[item[1]] = (max_read, vector_reads)
            elif item[0] == "max":
                diffs.append(item[1])
                blocks_read[item[1]] = (max_relu, len(diffs))
        turn_of = {item[2]: item[1] for item in plan if item[0] == "turn"}

        def first_of_pair(i):
            return i + 1

        def mode_part(engine, k2, lh, g, part):
            rows = slice(32 * g, 32 * g + 32)
            half = slice(lh * MODES, (lh + 1) * MODES)
            dst = xm[rows].rearrange("p (jh k l) (jl m) -> p jh k (l jl) m", jh=2, k=2, jl=2)[
                :, :, k2, half, 8 * g + 4 * part:8 * g + 4 * part + 4]
            v = tmp3[rows, 4, :].rearrange("p (jh k n b) -> p jh k n b", jh=2, k=2, b=B)[:, :, k2, half]
            u = tmp3[rows, 3, :].rearrange("p (jh k n b) -> p jh k n b", jh=2, k=2, b=B)[:, :, k2, half]
            return engine.tensor_tensor(dst, v, u, ALU.subtract if part else ALU.add)

        def xin_bank(n):
            return ps[0:96, (2 + n) % 8, :].rearrange("p (y x) -> p y x", x=W)

        def xin_slot(n):
            e, b = divmod(n, B)
            return xst[0:96, b, 16 * e * WP:16 * (e + 1) * WP].rearrange("p (y x) -> p y x", x=WP)[:, :, 1:1 + W]

        GN_STEPS = 3 + 3 + 6
        K_DIFF = 3 * GN_STEPS + 1
        K_RESID = K_DIFF + 2
        Q_RESID = (K_RESID + 1, K_RESID + 2)

        @block.sync
        def _(sp):
            for e in range(2):
                half = slice(e * HALF, (e + 1) * HALF)
                sp.dma_start(xa[:, half], x[:, half]).then_inc(x_loaded[e], 16)
            sp.dma_start(cst[:, 0:N_FIRST], consts[:, 0:N_FIRST]).then_inc(first_loaded, 16)
            def stack_tile(t, n0, n1, signal):
                maps_ = slice(SLOTS_PER_TILE * t, SLOTS_PER_TILE * (t + 1))
                for b in range(B):
                    sp.dma_start(stack[:, t % 3, b, n0:n1], maps[32 * b:32 * b + 32, maps_, n0:n1]
                                 ).then_inc(signal, 16)

            for cut, signal in enumerate((tile0_top, tile_in[0])):
                sp.wait_ge(act_map, 2 * cut + 2)
                sp.wait_ge(map_ready, 2 * cut + 2)
                stack_tile(0, *CUTS[cut], signal)
            for t in range(1, len(TILES)):
                sp.wait_ge(map_ready, SLOTS_PER_TILE * (t + 1))
                if t == 3:
                    sp.wait_ge(tile0_used, 1)
                stack_tile(t, 0, NP, tile_in[t])
            sp.dma_start(cst[:, N_FIRST:N_CONST], consts[:, N_FIRST:N_CONST]).then_inc(consts_loaded, 16)
            for s in range(PARTS):
                if s == 0:
                    sp.wait_ge(k_rounded, 1)
                    sp.wait_ge(k_zeroed, 2)
                if s < 2:
                    sp.wait_ge(part_act, 2 + s)
                else:
                    sp.wait_ge(part_dve, 1)
                sp.dma_start(k_dram[s].rearrange("c g n -> g c n"), k_parts[:, s, :]).then_inc(kd_written, 16)
            for s in range(PARTS):
                if s < 2:
                    sp.wait_ge(part_act, 4 + s)
                else:
                    sp.wait_ge(part_dve, 2)
                sp.dma_start(q_dram[s, 0].rearrange("c g n -> g c n"), q_parts[:, s, 0:HALF]
                             ).then_inc(qd_written[0], 16)

            def stack_k(i, g0, g1):
                src = k_dram[:, :, g0:g1, :].rearrange("t c g n -> (t c) (g n)")
                sp.dma_start(kst[0:PAIR_ROWS, g0:g1, :].rearrange("p g n -> p (g n)"),
                             src.unsqueeze(0).to_broadcast([PARTS, PARTS * HC, (g1 - g0) * KW])
                             ).then_inc(k_in[i], 16)

            def stack_q(i, e, g0, g1):
                for s in range(PARTS):
                    r0 = s * PARTS * HC
                    src = q_dram[s, e, :, g0:g1, :].rearrange("c g n -> c (g n)")
                    sp.dma_start(qst[r0:r0 + PARTS * HC, e, g0:g1, :].rearrange("p g n -> p (g n)"),
                                 src.unsqueeze(0).to_broadcast([PARTS, HC, (g1 - g0) * HALF])
                                 ).then_inc(q_in[i], 16)

            sp.wait_ge(k_padded, 1)
            sp.wait_ge(q_filled, 1)
            sp.wait_ge(kd_written, PARTS * 16)
            stack_k(0, 0, HEADS // 2)
            sp.wait_ge(qd_written[0], PARTS * 16)
            stack_q(0, 0, 0, HEADS)
            stack_k(1, HEADS // 2, HEADS)
            stack_q(1, 0, HEADS, G)
            stack_k(2, HEADS, G)
            sp.wait_ge(part_act, 7)
            sp.wait_ge(part_dve, 3)
            for s in range(PARTS):
                sp.dma_start(q_dram[s, 1].rearrange("c g n -> g c n"), q_parts[:, s, HALF:HW]
                             ).then_inc(qd_written[1], 16)
            for s in range(2 * B):
                e, b = divmod(s, B)
                sp.wait_ge(*blocks_read[turn_of[s]])
                sp.dma_start(qst[PAIR_ROWS:S_ROWS, e, b * HEADS:(b + 1) * HEADS, :].rearrange("p g n -> p (g n)"),
                             mt_sb[:]).then_inc(m_in, 16)
                if s == 0:
                    sp.wait_ge(qd_written[1], PARTS * 16)
                    stack_q(2, 1, 0, G)
                    sp.dma_start(wm, wmodes).then_inc(wm_loaded, 16)
            for e in range(2):
                half = slice(e * HALF, (e + 1) * HALF)
                sp.wait_ge(res_ready, e + 1)
                sp.dma_start(out[:, half], xb[:, half]).then_inc(stored, 16)
            sp.wait_ge(stored, 2 * 16)

        @block.gpsimd
        def _(pool):
            nc.gpsimd.memset(zeros[:], 0.0).then_inc(zeros_ready, 1)
            nc.gpsimd.memset(xp[:], 0.0).then_inc(xp_zeroed, 1)
            nc.gpsimd.memset(vt[:], 0.0).then_inc(vt_zeroed, 1)
            nc.gpsimd.memset(vrest[:], 0.0).then_inc(vt_zeroed, 1)
            pool.wait_ge(vt_zeroed, 2)
            pool.wait_ge(tile0_top, B * 16)
            for t in range(2):
                pool.wait_ge(tile_in[t], B * 16)
            nc.gpsimd.memset(arena_a[64:P, 0:q_words], 0.0).then_inc(q_filled, 1)
            pool.wait_ge(q_filled, 1)
            pool.wait_ge(l0_done, 1)
            nc.gpsimd.memset(xst[:], 0.0).then_inc(xst_zeroed, 1)
            pool.wait_ge(xst_zeroed, 1)
            pool.wait_ge(k_filled, 2)
            nc.gpsimd.memset(kst[64:P, :, KEYS:KPAD], 0.0).then_inc(k_padded, 1)
            pool.wait_ge(k_padded, 1)
            pool.wait_ge(l0_read, 2)
            nc.gpsimd.memset(k_parts[:, 0, KEYS:KPAD], 0.0).then_inc(k_zeroed, 1)
            nc.gpsimd.memset(k_res[:, KEYS:KPAD], 0.0).then_inc(k_zeroed, 1)
            pool.wait_ge(k_zeroed, 2)
            pool.wait_ge(xin_act, 2)
            pool.wait_ge(xin_dve, 2)
            nc.gpsimd.memset(xst[0:32, :, 0:WP], 0.0).then_inc(xin_ready, 1)
            pool.wait_ge(xin_act, 4)
            pool.wait_ge(xin_dve, 4)
            pool.wait_ge(xin_ready, 1)
            nc.gpsimd.memset(xst[64:96, :, (H - 1) * WP:H * WP], 0.0).then_inc(xin_ready, 1)
            pool.wait_ge(vt_ready, 2 + HEADS)
            pool.wait_ge(xin_ready, 2)
            nc.gpsimd.memset(vt[:, :, :, HC:HC + 1], 1.0).then_inc(vt_zeroed, 1)
            for h in range(HEADS):
                pool.wait_ge(vt_zeroed, 3 + h)
                nc.gpsimd.memset(vrest[32 * h:32 * h + KREST, :, 32 * h + HC:32 * h + HC + 1], 1.0
                                 ).then_inc(vt_zeroed, 1)
            for n in range(2 * B):
                pool.wait_ge(o_summed, n + 1)
                if n >= 2:
                    pool.wait_ge(attn_ready, n - 1)
                nc.gpsimd.tensor_tensor(on[:, n % 2, :].rearrange("p (a c) -> p a c", c=32),
                                        ot[:, n % 2, :].rearrange("p (a c) -> p a c", c=32),
                                        rden[:, n % 2, :, None].to_broadcast([P, 16, 32]),
                                        ALU.mult).then_inc(o_scaled, 1)
            pool.wait_ge(scored, 2 * B * EXP_UNITS)
            nc.gpsimd.memset(arena_a[:, 0:8192], 0.0).then_inc(xm_zeroed, 1)
            pool.wait_ge(tu_ready, 8)
            pool.wait_ge(xm_zeroed, 1)
            for i, stage in enumerate(MODE_STAGES):
                for g in range(POOL_MODES):
                    if i or g:
                        pool.wait_ge(xm_pool, i * POOL_MODES + g)
                    mode_part(nc.gpsimd, *stage, g, 1).then_inc(xm_pool, 1)

        @block.scalar
        def _(act):
            act.wait_ge(padded, 1)
            for n0, n1 in CUTS:
                nc.scalar.activation(maps[:, 0, n0:n1], xp[:, n0:n1], ACT.Copy).then_inc(act_map, 1)
                nc.scalar.activation(maps[:, 1, n0:n1], xp[:, n0:n1], ACT.Square, scale=VOLTERRA_SCALE ** 0.5
                                     ).then_inc(act_map, 1)
            act.wait_ge(l0_done, 1)
            act.wait_ge(planes_done, 1)
            nc.scalar.activation(planes[0:96, :].rearrange("p (a n) -> p a n", n=PLANE), ps[0:96, 2:5, 0:PLANE],
                                 ACT.Copy).then_inc(planes_ready, 1)
            act.wait_ge(consts_loaded, 16)
            act.wait_ge(xst_zeroed, 1)
            for n in range(0, 2 * B, 2):
                act.wait_ge(xin_done, n + 1)
                nc.scalar.activation(xin_slot(n), xin_bank(n), ACT.Identity, bias=c_("bin", 0, 96)
                                     ).then_inc(xin_act, 1)
            act.wait_ge(k_done, 2)
            nc.scalar.activation(k_first, ps[:, 2, 0:KHALF], ACT.Copy).then_inc(part_act, 1)
            nc.scalar.activation(k_parts[:, 0, 0:KEYS].rearrange("p (a n) -> p a n", a=2),
                                 ps[:, 2:4, 0:KHALF], ACT.Copy).then_inc(k_rounded, 1)
            act.wait_ge(dve_step, K_DIFF)
            nc.scalar.activation(k_parts[:, 0, KDIFF:KW], k_res[:, KDIFF:KW], ACT.Copy).then_inc(part_act, 1)
            act.wait_ge(dve_step, K_RESID)
            act.wait_ge(k_zeroed, 2)
            nc.scalar.activation(k_parts[:, 1, :], k_res, ACT.Copy).then_inc(part_act, 1)
            for e in range(2):
                half = slice(e * HALF, (e + 1) * HALF)
                act.wait_ge(q_done, e + 1)
                nc.scalar.activation(q_parts[:, 0, half], ps[:, 4 + e, :], ACT.Copy).then_inc(part_act, 1)
                act.wait_ge(dve_step, Q_RESID[e])
                nc.scalar.activation(q_parts[:, 1, half], q_res[:, half], ACT.Copy).then_inc(part_act, 1)
            act.wait_ge(v_done, 2)
            nc.scalar.activation(vs.rearrange("p (a n) -> p a n", a=2), ps[:, 6:8, 0:KHALF],
                                 ACT.Copy).then_inc(vs_ready, 1)
            for item in plan:
                if item[0] == "score":
                    n = item[1]
                    act.wait_ge(scored, n + 1)
                    if n >= PRING:
                        old_half, old = divmod(n - PRING, EXP_UNITS)
                        act.wait_ge(pv_done, 2 * (old_half * (DT + 1) + old // HEADS + 1))
                    nc.scalar.activation(probs[:, n % PRING, :], ps[:, SCORE_RING[n % len(SCORE_RING)], :], ACT.Exp).then_inc(expd, 1)
                elif item[0] == "max" and item[4] == "diff":
                    i = item[1]
                    d = diffs.index(i)
                    act.wait_ge(max_scored, i + 1)
                    if d >= 3:
                        act.wait_ge(*blocks_read[first_of_pair(diffs[d - 3])])
                    nc.scalar.activation(relus[:, d % 3, :], ps[:, block_bank(i), 0:KHALF], ACT.Relu
                                         ).then_inc(max_relu, 1)
                elif item[0] == "gates":
                    e = item[1]
                    act.wait_ge(gb_ready, 1)
                    for i in range(3):
                        act.wait_ge(gate_done, 3 * e + i + 1)
                        nc.scalar.activation(tmp3[:, i, e * HALF:(e + 1) * HALF], ps[:, GATE_BANKS[i], :], ACT.Tanh,
                                             bias=gb[:, i:i + 1], scale=1.0 if i == 1 else 0.5).then_inc(gate_act, 1)
                elif item[0] == "cell":
                    e = item[1]
                    act.wait_ge(cell_ready, e + 1)
                    nc.scalar.activation(tmp3[:, 4, e * HALF:(e + 1) * HALF], tmp3[:, 3, e * HALF:(e + 1) * HALF],
                                         ACT.Tanh, scale=0.5).then_inc(cell_act, 1)

        @block.vector
        def _(dve):
            chain = [0]

            def link(ins):
                chain[0] += 1
                ins.then_inc(dve_step, 1)
                dve.wait_ge(dve_step, chain[0])

            def norm(src, dst):
                link(nc.vector.bn_stats(stats[:, 0:6], src[:, 0:HALF]))
                link(nc.vector.bn_stats(stats[:, 6:12], src[:, HALF:HW]))
                return norm_from_stats(src, dst)

            def norm_from_stats(src, dst):
                link(nc.vector.bn_aggr(small[:, 0:2], stats[:, :].rearrange("p (a b) -> p a b", b=6)))
                mean, var, v, y, t, nh = (small[:, i:i + 1] for i in range(6))
                link(nc.vector.tensor_scalar(v, var, EPS, None, ALU.add))
                link(nc.vector.tensor_scalar(y.bitcast(I32), v.bitcast(I32), -0.5, float(0x5F3759DF),
                                             ALU.mult, ALU.add))
                link(nc.vector.tensor_scalar(nh, v, -0.5, None, ALU.mult))
                for _ in range(3):
                    link(nc.vector.scalar_tensor_tensor(t, y, nh, y, ALU.mult, ALU.mult))
                    link(nc.vector.scalar_tensor_tensor(y, t, 1.5, y, ALU.add, ALU.mult))
                return nc.vector.tensor_scalar(dst, src3(src, dst), mean, y, ALU.subtract, ALU.mult)

            def src3(src, dst):
                return src.rearrange("p (y x) -> p y x", x=W) if len(dst.shape) == 3 else src

            for e in range(2):
                dve.wait_ge(x_loaded[e], 16)
                link(nc.vector.bn_stats(stats[:, 6 * e:6 * e + 6], xa[:, e * HALF:(e + 1) * HALF]))
            dve.wait_ge(xp_zeroed, 1)
            norm_from_stats(xa[:], interior(xp)).then_inc(padded, 1)
            dve.wait_ge(padded, 1)
            order = [(SLOTS_PER_TILE * t + i, d, sy * WP + sx) for t, (maps_, _) in enumerate(TILES)
                     for i, (d, (sy, sx)) in enumerate(maps_)]
            steps = [(n0, n1, *step) for n0, n1 in CUTS for step in order[2:4]]
            steps += [(0, NP, *step) for step in order[4:]]
            for n0, n1, m, (dy, dx), pre in steps:
                at = dy * WP + dx + pre
                nc.vector.scalar_tensor_tensor(maps[:, m, n0:n1], xp[:, pre + n0:pre + n1], VOLTERRA_SCALE,
                                               xp[:, at + n0:at + n1], ALU.mult, ALU.mult).then_inc(map_ready, 1)
            dve.wait_ge(tile0_top, B * 16)
            last_tile = (N_MAPS - 4) * NP
            for t, (w0, w1) in ((2, (q_words, last_tile)), (3, (last_tile, q_words + k_words))):
                for tile in range(t + 1):
                    dve.wait_ge(tile_in[tile], B * 16)
                nc.vector.memset(arena_a[64:P, w0:w1], TWO_ONES).then_inc(k_filled, 1)
            dve.wait_ge(l0_done, 1)
            dve.wait_ge(first_loaded, 16)
            l0t = stack[:, 2, 0, 0:HW]
            nc.vector.transpose(l0t.rearrange("p (j o) -> p j o", o=32),
                                banks(0).rearrange("p (i j) -> p j i", j=32)).then_inc(l0_read, 1)
            dve.wait_ge(l0_read, 1)
            nc.vector.scalar_tensor_tensor(xb[:], l0t, c_("l0bias"), xa[:], ALU.add, ALU.add).then_inc(l0_read, 1)
            dve.wait_ge(l0_read, 2)
            dve.wait_ge(act_map, 4)
            norm(xb[:], interior(xp)).then_inc(padded, 1)
            dve.wait_ge(consts_loaded, 16)
            dve.wait_ge(l1s_done, 1)
            for px in range(3):
                nc.vector.tensor_tensor(
                    l1s[:, px, :].rearrange("p (b o) -> p b o", b=B),
                    ps[0:96, 7, px * 32:(px + 1) * 32].unsqueeze(1).to_broadcast([96, B, 32]),
                    c_("dmask", 0, 96).unsqueeze(2).to_broadcast([96, B, 32]), ALU.mult).then_inc(l1s_ready, 1)
            for e in range(2):
                half = slice(e * HALF, (e + 1) * HALF)
                dve.wait_ge(l1_done, e + 1)
                nc.vector.scalar_tensor_tensor(xc[:, half], ps[:, e, :], c_("l1bias"), xb[:, half], ALU.add, ALU.add
                                               ).then_inc(l1_read, 1)
                dve.wait_ge(l1_read, e + 1)
                link(nc.vector.bn_stats(stats[:, 6 * e:6 * e + 6], xc[:, half]))
            dve.wait_ge(planes_done, 1)
            norm_from_stats(xc[:], interior(xp)).then_inc(padded, 1)
            dve.wait_ge(padded, 3)
            dve.wait_ge(xst_zeroed, 1)
            for n in range(1, 2 * B, 2):
                dve.wait_ge(xin_done, n + 1)
                nc.vector.tensor_scalar(xin_slot(n), xin_bank(n), c_("bin", 0, 96), None, ALU.add
                                        ).then_inc(xin_dve, 1)
            nc.vector.tensor_scalar(xb[:], xc[:], c_("bout"), None, ALU.add).then_inc(l1_read, 1)
            nc.vector.tensor_copy(ident_b[:], c_("ident")).then_inc(l1_read, 1)
            nc.vector.memset(mx[:], -3.0e38).then_inc(l1_read, 1)
            rows = xp[:, WP:WP + 32 * WP].rearrange("p (y x) -> p y x", x=WP)
            for v in range(3):
                nc.vector.tensor_reduce(wsum[:, v, :], rows[:, :, 1 + v:1 + v + KH], AX.X, ALU.add
                                        ).then_inc(win_ready, 1)
            dve.wait_ge(win_ready, 3)
            for u in range(3):
                nc.vector.tensor_reduce(win9[:, 0, 3 * u:3 * u + 3], wsum[:, :, u:u + KH], AX.X, ALU.add
                                        ).then_inc(win_ready, 1)
            dve.wait_ge(part_act, 1)
            dve.wait_ge(k_rounded, 1)
            link(nc.vector.tensor_tensor(k_res[:, KDIFF:KW], ps[:, 3, 0:KHALF], k_first, ALU.subtract))
            assert chain[0] == K_DIFF
            link(nc.vector.tensor_tensor(k_res[:, 0:KEYS].rearrange("p (a n) -> p a n", a=2),
                                         ps[:, 2:4, 0:KHALF],
                                         k_parts[:, 0, 0:KEYS].rearrange("p (a n) -> p a n", a=2),
                                         ALU.subtract))
            dve.wait_ge(part_act, 2)
            link(nc.vector.tensor_tensor(k_res[:, KDIFF:KW], k_res[:, KDIFF:KW], k_parts[:, 0, KDIFF:KW],
                                         ALU.subtract))
            assert chain[0] == K_RESID
            dve.wait_ge(win_done, 1)
            nc.vector.tensor_scalar(win9[:, 1, :], ps[:, 0, 16:25], 1.0 / KEYS, c_("bin"), ALU.mult, ALU.add
                                    ).then_inc(win_scaled, 1)
            dve.wait_ge(part_act, 3)
            nc.vector.tensor_tensor(k_parts[:, 2, :], k_res, k_parts[:, 1, :], ALU.subtract).then_inc(part_dve, 1)
            for e in range(2):
                half = slice(e * HALF, (e + 1) * HALF)
                dve.wait_ge(part_act, 4 + 2 * e)
                link(nc.vector.tensor_tensor(q_res[:, half], ps[:, 4 + e, :], q_parts[:, 0, half], ALU.subtract))
                assert chain[0] == Q_RESID[e]
                if e == 1:
                    dve.wait_ge(a2_done, 1)
                    nc.vector.tensor_copy(a2[:], ps[:, 0, 0:1]).then_inc(a2_ready, 1)
                dve.wait_ge(part_act, 5 + 2 * e)
                nc.vector.tensor_tensor(q_parts[:, 2, half], q_res[:, half], q_parts[:, 1, half], ALU.subtract
                                        ).then_inc(part_dve, 1)
            dve.wait_ge(gb_done, 1)
            link(nc.vector.tensor_tensor(gb[:], ps[:, 0, 8:11], c_("gbias"), ALU.add))
            for i in (0, 2):
                nc.vector.tensor_scalar(gb[:, i:i + 1], gb[:, i:i + 1], 0.5, None, ALU.mult).then_inc(gb_ready, 1)
            dve.wait_ge(vt_zeroed, 2)
            dve.wait_ge(vt_done, 1)
            nc.vector.tensor_copy(vt[:, 0:4, :, 0:HC],
                                  ps[:, 0, :].rearrange("p (t g c) -> p t g c", t=4, c=HC)).then_inc(vt_ready, 1)
            dve.wait_ge(vt_done, 2)
            nc.vector.tensor_copy(vt[:, 4:DT, :, 0:HC],
                                  ps[:, 1, 0:(DT - 4) * P].rearrange("p (t g c) -> p t g c", t=DT - 4, c=HC)
                                  ).then_inc(vt_ready, 1)
            for h in range(HEADS):
                r = slice(32 * h, 32 * h + KREST)
                nc.vector.tensor_copy(vrest[r, :, 32 * h:32 * h + HC],
                                      ps[r, 1, 3 * P:4 * P].rearrange("p (b h c) -> p b h c", h=HEADS, c=HC)[:, :, h, :]
                                      ).then_inc(vt_ready, 1)

            def split_max(b):
                dve.wait_ge(max_read, split_after[b])
                link(nc.vector.tensor_reduce(negm[:, 0, :], mx[:], AX.X, ALU.max, negate=True))
                if b > 0:
                    dve.wait_ge(max_scored, turn_of[b - 1] + 1)
                link(nc.vector.tensor_copy(mparts[:, 0, :], negm[:, 0, :]))
                link(nc.vector.tensor_tensor(negm[:, 1, :], negm[:, 0, :], mparts[:, 0, :], ALU.subtract))
                link(nc.vector.tensor_copy(mparts[:, 1, :], negm[:, 1, :]))
                nc.vector.tensor_tensor(mparts[:, 2, :], negm[:, 1, :], mparts[:, 1, :], ALU.subtract
                                        ).then_inc(m_split, 1)

            dve.wait_ge(l1_read, 5)
            pairs = 0
            for item in plan:
                if item[0] == "max" and item[4] != "diff":
                    _, i, b, a, kind = item
                    dve.wait_ge(max_scored, i + 1)
                    bank = ps[:, block_bank(i), 0:KHALF]
                    if i - 1 in diffs:
                        d = diffs.index(i - 1)
                        dve.wait_ge(max_relu, d + 1)
                        if d >= 2:
                            dve.wait_ge(*blocks_read[first_of_pair(diffs[d - 2])])
                        nc.vector.tensor_tensor_reduce(out=sums[:, d % 2, :], in0=bank, in1=relus[:, d % 3, :],
                                                       scale=1.0, scalar=-3.0e38, op0=ALU.add, op1=ALU.max,
                                                       accum_out=mx[:, a, 0:1]).then_inc(max_read, 1)
                    else:
                        e = 0 if kind == "first" else 1
                        nc.vector.tensor_reduce(mx[:, a, e:e + 1], bank, AX.X, ALU.max).then_inc(max_read, 1)
                elif item[0] == "split":
                    split_max(item[1])
                elif item[0] == "turn":
                    _, i, b = item
                    dve.wait_ge(max_scored, i + 1)
                    if b > 0:
                        dve.wait_ge(m_in, 16 * b)
                    nc.vector.tensor_copy(mt_sb[:], ps[0:PARTS * ROWS_OF_MAX, block_bank(i), 0:P // 2].bitcast(BF16)
                                          ).then_inc(max_read, 1)
                elif item[0] == "read":
                    n = item[1]
                    dve.wait_ge(pv_done, 2 * (n + 1) * (DT + 1))
                    if n >= 2:
                        dve.wait_ge(o_scaled, n - 1)
                    nc.vector.transpose(ot[:, n % 2, :], ps[:, O_RING[n % len(O_RING)], :]).then_inc(o_read, 1)
                    dve.wait_ge(o_read, n + 1)
                    nc.vector.reciprocal(rden[:, n % 2, :, None],
                                         ot[:, n % 2, :].rearrange("p (a c) -> p a c", c=32)[:, :, HC:HC + 1]
                                         ).then_inc(o_summed, 1)
                elif item[0] == "write":
                    n = item[1]
                    dve.wait_ge(o_scaled, n + 1)
                    e, b = divmod(n, B)
                    nc.vector.transpose(attn[:, b, e * HALF:(e + 1) * HALF], on[:, n % 2, :]
                                        ).then_inc(attn_ready, 1)
                elif item[0] == "cell":
                    e = item[1]
                    half = slice(e * HALF, (e + 1) * HALF)
                    dve.wait_ge(gate_act, 3 * e + 2)
                    nc.vector.scalar_tensor_tensor(tmp3[:, 3, half], tmp3[:, 0, half], 1.0, tmp3[:, 1, half],
                                                   ALU.add, ALU.mult).then_inc(cell_ready, 1)
                elif item[0] == "hidden":
                    e = item[1]
                    half = slice(e * HALF, (e + 1) * HALF)
                    dve.wait_ge(gate_act, 3 * e + 3)
                    dve.wait_ge(cell_act, e + 1)
                    nc.vector.scalar_tensor_tensor(tmp3[:, 5, half], tmp3[:, 2, half], 1.0, tmp3[:, 4, half],
                                                   ALU.add, ALU.mult).then_inc(h_ready, 1)
                elif item[0] == "out":
                    e = item[1]
                    half = slice(e * HALF, (e + 1) * HALF)
                    dve.wait_ge(wout_done, e + 1)
                    nc.vector.scalar_tensor_tensor(xc[:, half], ps[:, OUT_BANK, :], 0.5, xb[:, half],
                                                   ALU.mult, ALU.add).then_inc(x3_ready, 1)
                    dve.wait_ge(x3_ready, e + 1)
                    link(nc.vector.bn_stats(stats[:, 6 * e:6 * e + 6], xc[:, half]))
            link(norm_from_stats(xc[:], xa[:]))
            for e in range(2):
                nc.vector.transpose(tmp3[:, 0, e * HALF:(e + 1) * HALF].rearrange("p (w c) -> p w c", c=C),
                                    xa[:, :].rearrange("p (h w) -> p w h", w=W)[:, e * W // 2:(e + 1) * W // 2]
                                    ).then_inc(t1_ready, 1)
            for i in range(2):
                dve.wait_ge(rows_done, i + 1)
                nc.vector.transpose(tmp3[:, 1 + i, :].rearrange("p (c k) -> p c k", k=MODES),
                                    banks(2 * i).rearrange("p (w c) -> p c w", c=C)).then_inc(t2_ready, 1)
            for i in range(2):
                src = banks(4 + 2 * i).rearrange("p (b c k jl) -> p b k jl c", b=B, c=C, jl=2)
                dst = tmp3[:, 3 + i, :].rearrange("p (k l jl b) -> p b k jl l", b=B, l=MODES, jl=2)
                for b in range(B):
                    if b % 2 == 0:
                        dve.wait_ge(cols_done, 2 * i + b // 2 + 1)
                    nc.vector.transpose(dst[:, b], src[:, b]).then_inc(tu_ready, 1)
            dve.wait_ge(tu_ready, 8)
            dve.wait_ge(xm_zeroed, 1)
            for stage in MODE_STAGES:
                for g in range(4):
                    mode_part(nc.vector, *stage, g, 0).then_inc(xm_dve, 1)
                    if g >= POOL_MODES:
                        mode_part(nc.vector, *stage, g, 1).then_inc(xm_dve, 1)
            for k2 in range(2):
                dve.wait_ge(mix_done, k2 + 1)
                for jl in range(2):
                    nc.vector.transpose(
                        y1[:, (2 * k2 + jl) * HW:(2 * k2 + jl + 1) * HW].rearrange("p (o m) -> p o m", m=32),
                        banks(4 * k2, 4).rearrange("p (l j o) -> p j o l", j=2, o=C)[:, jl]).then_inc(y1_ready, 1)
            for s in range(2):
                dve.wait_ge(inv_l_done, s + 1)
                nc.vector.transpose(z1[:, s * HW:(s + 1) * HW].rearrange("p (o h l) -> p o h l", h=2, l=16),
                                    ps[:, 4 + 2 * s:6 + 2 * s, :].rearrange("p h (o k) -> p o h k", o=C)
                                    ).then_inc(z1_ready, 1)
            for e in range(2):
                dve.wait_ge(inv_k_done, e + 1)
                link(nc.vector.transpose(
                    tmp3[:, 0, :].rearrange("p (k l) -> p l k", l=W)[:, e * W // 2:(e + 1) * W // 2],
                    ps[:, e, :].rearrange("p (o l) -> p l o", o=C)))
            for e in range(2):
                half = slice(e * HALF, (e + 1) * HALF)
                nc.vector.scalar_tensor_tensor(xb[:, half], tmp3[:, 0, half], 0.5 / HW, xc[:, half],
                                               ALU.mult, ALU.add).then_inc(res_ready, 1)

        @block.tensor
        def _(pe):
            mm = nc.tensor.matmul

            def keep_clock(bank, n):
                for _ in range(n):
                    mm(ps[:, bank, :], zeros[:, 0:P], zeros[:], start=True, stop=True)

            pe.wait_ge(zeros_ready, 1)
            pe.wait_ge(x_loaded[0], 16)
            keep_clock(7, WARM_L0)
            for n in (1, 3, 5, 6):
                pe.wait_ge(map_ready, n)
                keep_clock(7, WARM_MAP)
            l0w = c_("l0w").rearrange("p (s o) -> p s o", o=32)
            pe.wait_ge(first_loaded, 16)
            for e in range(2):
                rows = [slice(32 * b, 32 * b + 32) for b in range(B)]
                for s, (t, (py, px)) in enumerate(SLOTS):
                    if t == 0:
                        if s == 0:
                            pe.wait_ge(tile_in[0] if e else tile0_top, B * 16)
                        for b in range(B):
                            last = mm(ps[rows[b], e, :].rearrange("p (y x) -> p y x", x=W), l0w[:, s, :],
                               window(stack[:, 0, b, :], py, px, 16 * e, 16, W), start=(s == 0), stop=False,
                               skip_group_check=True)
            last.then_inc(tile0_used, 1)
            for s, (t, (py, px)) in enumerate(SLOTS):
                if t == 0:
                    continue
                if SLOTS[s - 1][0] != t:
                    pe.wait_ge(tile_in[t], B * 16)
                for e in range(2):
                    for b in range(B):
                        last = mm(ps[32 * b:32 * b + 32, e, :].rearrange("p (y x) -> p y x", x=W), l0w[:, s, :],
                                  window(stack[:, t % 3, b, :], py, px, 16 * e, 16, W), start=False,
                                  stop=(s == len(SLOTS) - 1), skip_group_check=True)
            last.then_inc(l0_done, 1)

            pe.wait_ge(consts_loaded, 16)
            mm(ps[0:96, 7, 0:96], c_("ones", 0, 96)[:, 0:96], c_("l1w", 0, 96), start=True, stop=True
               ).then_inc(l1s_done, 1)
            keep_clock(6, W1)
            pe.wait_ge(l0_read, 1)
            keep_clock(6, W2)
            pe.wait_ge(l0_read, 2)
            keep_clock(6, W3)
            pe.wait_ge(padded, 2)
            for i in range(3):
                for r in range(3):
                    at = r * WP + i * PLANE
                    last = mm(ps[32 * r:32 * r + 32, 2 + i, 0:PLANE], c_("bsel"), xp[:, at:at + PLANE],
                              start=True, stop=True)
            last.then_inc(planes_done, 1)
            keep_clock(6, W4)
            pe.wait_ge(planes_ready, 1)
            pe.wait_ge(l1s_ready, 3)
            pe.wait_ge(l0_read, 1)
            for e in range(2):
                for px in range(3):
                    last = mm(ps[:, e, :].rearrange("p (y x) -> p y x", x=W), l1s[:, px, :],
                              window(planes[0:96, :], 0, px, 16 * e, 16, W), start=(px == 0), stop=(px == 2))
                last.then_inc(l1_done, 1)

            keep_clock(6, W5)
            pe.wait_ge(l1_read, 2)
            keep_clock(6, W6)
            pe.wait_ge(padded, 3)
            for n in range(2 * B):
                e, b = divmod(n, B)
                if n == 6:
                    pe.wait_ge(l1_read, 2)
                for r in range(3):
                    last = mm(ps[32 * r:32 * r + 32, (2 + n) % 8, :].rearrange("p (y x) -> p y x", x=W),
                              c_("win")[:, 32 * b:32 * b + 32],
                              window(xp, r, 1, 16 * e, 16, W), start=True, stop=True)
                last.then_inc(xin_done, 1)

            def conv(bank, weights, rows, cols, first, signal):
                ny = rows // 2
                for e in range(2):
                    pe.wait_ge(xin_ready, e + 1)
                    for px in range(3):
                        for b in range(B):
                            last = mm(ps[32 * b:32 * b + 32, bank + e, 0:ny * cols].rearrange("p (y x) -> p y x", x=cols),
                                      weights[:, px, :],
                                      window(xst[:, b, :], first, first + px, ny * e, ny, cols),
                                      start=(px == 0), stop=(px == 2))
                    last.then_inc(signal, 1)

            qkv = c_("qkv").rearrange("p (a s o) -> p a s o", a=3, o=32)
            images = [slice(32 * b, 32 * b + 32) for b in range(B)]
            conv(2, qkv[:, 1], KH, KH, 1, k_done)
            pe.wait_ge(win_ready, 6)
            mm(ps[:, 0, 16:25], c_("win"), win9[:, 0, :], start=True, stop=True).then_inc(win_done, 1)
            conv(4, qkv[:, 0], H, W, 0, q_done)
            pe.wait_ge(win_scaled, 1)
            v2w = c_("v2w").rearrange("p (s o) -> p s o", o=32)
            for r in images:
                for s in range(9):
                    last = mm(ps[r, 0, 0:1], v2w[r, s, :], win9[r, 1, s:s + 1], start=(s == 0), stop=(s == 8))
            last.then_inc(a2_done, 1)
            conv(6, qkv[:, 2], KH, KH, 1, v_done)
            pe.wait_ge(a2_ready, 1)
            proj2 = c_("proj2").rearrange("p (s o) -> p s o", o=32)
            for r in images:
                for i in range(3):
                    last = mm(ps[r, 0, 8 + i:9 + i], proj2[r, i, :], a2[r, :], start=True, stop=True)
            last.then_inc(gb_done, 1)
            pe.wait_ge(vs_ready, 1)
            pe.wait_ge(gb_ready, 2)
            for t in range(DT):
                last = nc.tensor.transpose(ps[:, t // 4, (t % 4) * P:(t % 4 + 1) * P],
                                           vs[:, t * P:(t + 1) * P], c_("ident"))
                if t == 3:
                    last.then_inc(vt_done, 1)
            for h in range(HEADS):
                last = mm(ps[32 * h:32 * h + KREST, 1, 3 * P:4 * P], vs[:, DT * P:KEYS], c_("ident"),
                          start=True, stop=True)
            last.then_inc(vt_done, 1)

            pe.wait_ge(part_dve, 3)
            keep_clock(2, W8)
            def max_block(i, s, a, kind):
                before = block_before(i, block_bank(i))
                if before is not None:
                    pe.wait_ge(*blocks_read[before])
                e, b = divmod(s, B)
                h, qt = divmod(a, HALF_TILES)
                g = b * HEADS + h
                at = {"first": 0, "second": KHALF, "diff": KDIFF}[kind]
                mm(ps[:, block_bank(i), 0:KHALF], qst[:, e, g, qt * P:(qt + 1) * P], kst[:, g, at:at + KHALF],
                   start=True, stop=True).then_inc(max_scored, 1)

            def turn_maxima(i, s):
                pe.wait_ge(*blocks_read[block_before(i, block_bank(i))])
                pe.wait_ge(m_split, s + 1)
                nc.tensor.transpose(ps[0:PARTS * ROWS_OF_MAX, block_bank(i), 0:P // 2].bitcast(BF16),
                                    mparts[:].rearrange("p s n -> p (s n)"), ident_b[:]).then_inc(max_scored, 1)

            def score_tile(n):
                half, i = divmod(n, EXP_UNITS)
                e, b = divmod(half, B)
                if i == 0:
                    pe.wait_ge(m_in, 16 * (half + 1))
                bank = SCORE_RING[n % len(SCORE_RING)]
                if n >= len(SCORE_RING):
                    pe.wait_ge(expd, n - len(SCORE_RING) + 1)
                else:
                    pe.wait_ge(*blocks_read[block_before(prologue, bank)])
                if i < HEADS * DT:
                    t, h = divmod(i, HEADS)
                    g = b * HEADS + h
                    last = mm(ps[:, bank, :], kst[:, g, t * P:(t + 1) * P], qst[:, e, g, :],
                              start=True, stop=True)
                else:
                    for h in range(HEADS):
                        g = b * HEADS + h
                        last = mm(ps[32 * h:32 * h + 32, bank, :], kst[:, g, DT * P:KPAD],
                                  qst[:, e, g, :], start=True, stop=True)
                last.then_inc(scored, 1)

            def values(half, t, c):
                n0 = half * EXP_UNITS + t * HEADS
                cols = slice(c * HALF // 2, (c + 1) * HALF // 2)
                bank = O_RING[half % len(O_RING)]
                if t == 0 and c == 0 and half >= len(O_RING):
                    pe.wait_ge(o_read, half - len(O_RING) + 1)
                if t < DT:
                    pe.wait_ge(expd, n0 + HEADS)
                    for h in range(HEADS):
                        last = mm(ps[32 * h:32 * h + 32, bank, cols], vt[:, t, half % B * HEADS + h, :],
                                  probs[:, (n0 + h) % PRING, cols], start=(t == 0 and c == 0), stop=False,
                                  skip_group_check=True)
                else:
                    pe.wait_ge(expd, n0 + 1)
                    last = mm(ps[:, bank, cols], vrest[:, half % B, :], probs[:, n0 % PRING, cols], start=False,
                              stop=(c == 1), skip_group_check=True)
                last.then_inc(pv_done, 1)

            proj = c_("proj").rearrange("p (s o) -> p s o", o=32)
            pe.wait_ge(k_in[0], 16)
            pe.wait_ge(q_in[0], PARTS * 16)
            pe.wait_ge(vt_ready, 2 + HEADS)
            for item in plan:
                if item[0] == "max":
                    if item[2:5] == (0, ROWS_OF_MAX // 2, "diff"):
                        pe.wait_ge(k_in[1], 16)
                    elif item[2:5] == (1, 0, "diff"):
                        pe.wait_ge(k_in[2], 16)
                        pe.wait_ge(q_in[1], PARTS * 16)
                    elif item[2:5] == (B, 0, "diff"):
                        pe.wait_ge(q_in[2], PARTS * 16)
                    max_block(*item[1:])
                elif item[0] == "turn":
                    turn_maxima(*item[1:])
                elif item[0] == "score":
                    if item[1] == 0:
                        pe.wait_ge(vt_zeroed, 3 + HEADS)
                    score_tile(item[1])
                elif item[0] == "values":
                    values(*item[1:])

                elif item[0] == "gates":
                    e = item[1]
                    if e == 0:
                        pe.wait_ge(*blocks_read[turn_of[2 * B - 1]])
                        pe.wait_ge(*blocks_read[turn_of[2 * B - 1] - 1])
                        pe.wait_ge(*blocks_read[turn_of[2 * B - 1] - 2])
                    else:
                        pe.wait_ge(x3_ready, 1)
                        keep_clock(O_RING[0], W9)
                    pe.wait_ge(attn_ready, (e + 1) * B)
                    for i in range(3):
                        for b in range(B):
                            last = mm(ps[32 * b:32 * b + 32, GATE_BANKS[i], :], proj[:, i, :],
                                      attn[:, b, e * HALF:(e + 1) * HALF], start=True, stop=True)
                        last.then_inc(gate_done, 1)
                elif item[0] == "out":
                    e = item[1]
                    if e == 1:
                        keep_clock(O_RING[0], W10)
                    pe.wait_ge(h_ready, e + 1)
                    mm(ps[:, OUT_BANK, :], c_("wout"), tmp3[:, 5, e * HALF:(e + 1) * HALF], start=True, stop=True
                       ).then_inc(wout_done, 1)

            pe.wait_ge(x3_ready, 2)
            keep_clock(7, W7)
            for i, m in enumerate(("mt", "mrt")):
                for e in range(2):
                    pe.wait_ge(t1_ready, e + 1)
                    last = mm(ps[:, 2 * i + e, :], c_(m), tmp3[:, 0, e * HALF:(e + 1) * HALF], start=True, stop=True)
                last.then_inc(rows_done, 1)
            pe.wait_ge(x3_ready, 2)
            for i, m in enumerate(("mt", "mrt")):
                pe.wait_ge(t2_ready, i + 1)
                src = tmp3[:, 1 + i, :].rearrange("p (c k) -> p c k", k=MODES)
                for b in range(B):
                    for g in range(4):
                        dst = ps[32 * g:32 * g + 32, 4 + 2 * i + b // 2, (b % 2) * 256:(b % 2 + 1) * 256]
                        last = mm(dst.rearrange("p (c k) -> p c k", k=KG), c_(m)[:, 32 * b:32 * b + 32],
                                  src[:, :, KG * g:KG * (g + 1)], start=True, stop=True)
                    if b % 2:
                        last.then_inc(cols_done, 1)
            keep_clock(3, W11)
            pe.wait_ge(wm_loaded, 16)
            xv = xm.rearrange("p (jh k l) m -> p k l jh m", jh=2, k=2)
            wv = wm.rearrange("p (jh k l m) -> p k l jh m", jh=2, k=2, m=2 * C)
            for i, (k2, lh) in enumerate(MODE_STAGES):
                pe.wait_ge(xm_dve, (i + 1) * (8 - POOL_MODES))
                pe.wait_ge(xm_pool, (i + 1) * POOL_MODES)
                for l in range(lh * MODES // 2, (lh + 1) * MODES // 2):
                    for jh in range(2):
                        last = mm(banks(4 * k2, 4)[64 * jh:64 * jh + 64, 64 * l:64 * l + 64], xv[:, k2, l, jh],
                                  wv[:, k2, l, jh], start=True, stop=True)
                if lh == 1:
                    last.then_inc(mix_done, 1)
            yv = y1.rearrange("p (k jl o g s b) -> p s b jl o g k", k=2, jl=2, o=C, g=4, s=2)
            pe.wait_ge(y1_ready, 2)
            keep_clock(0, W12)
            pe.wait_ge(y1_ready, 4)
            for s, m in enumerate(("mt", "mnt")):
                for jh in range(2):
                    zv = ps[:, 4 + 2 * s + jh, :].rearrange("p (o g k j) -> p j o g k", g=4, j=2, k=2)
                    for jl in range(2):
                        j = 2 * jh + jl
                        for b in range(B):
                            last = mm(zv[32 * b:32 * b + 32, jl], c_(m)[:, 32 * j:32 * j + 32], yv[:, s, b, jl],
                                      start=(jl == 0), stop=True, skip_group_check=True)
                last.then_inc(inv_l_done, 1)
            for s in range(2):
                pe.wait_ge(z1_ready, s + 1)
                zs = z1[:, s * HW:(s + 1) * HW].rearrange("p (o l) -> p o l", l=W)
                for e in range(2):
                    last = mm(ps[:, e, :].rearrange("p (o l) -> p o l", o=C), c_(("mt_back", "mnt_back")[s]),
                              zs[:, :, e * W // 2:(e + 1) * W // 2], start=(s == 0), stop=(s == 1))
                    if s == 1:
                        last.then_inc(inv_k_done, 1)



def transform_matrix(n):
    if n == 1:
        return np.ones((1, 1), np.float32)
    m = transform_matrix(n // 2)
    k = np.arange(n // 2)
    cas = (np.cos(2 * np.pi * k / n) + np.sin(2 * np.pi * k / n)).astype(np.float32)[:, None]
    even = np.zeros((n // 2, n), np.float32)
    even[:, 0::2] = m
    odd = np.zeros((n // 2, n), np.float32)
    odd[:, 1::2] = m
    return np.concatenate([even + cas * odd, even - cas * odd], axis=0)


def blocks(m):
    out = np.zeros((P, P), np.float32)
    for b in range(B):
        out[32 * b:32 * b + 32, 32 * b:32 * b + 32] = m
    return out


def layout_consts(i):
    c = np.zeros((P, N_CONST), np.float32)

    def put(name, value, rows=P):
        at, n = CONSTS[name]
        c[0:rows, at:at + n] = np.asarray(value).reshape(rows, n)

    w1 = np.asarray(i["L0_conv_W1"]).reshape(C, 9, 32)
    w2 = np.asarray(i["L0_conv_W2"]).reshape(C, 9, 9, 32)
    l0 = np.zeros((C, 4, len(SLOTS), 32), np.float32)
    for s, (t, (py, px)) in enumerate(SLOTS):
        for slot, (d, pre) in enumerate(TILES[t][0]):
            pair = tap_pair(d, pre, py, px)
            if pair:
                l0[:, slot, s, :] = w1[:, pair[0]] if d is LINEAR else w2[:, pair[0], pair[1]]
    put("l0w", l0)
    put("l0bias", np.tile(np.asarray(i["L0_conv_bias_w"]).reshape(32), B))
    put("l1w", np.asarray(i["L1_conv_weight"])[:, :, ::-1, ::-1].transpose(2, 1, 3, 0), 96)
    bsel = np.zeros((B, C, 32), np.float32)
    dmask = np.zeros((4, 32, B), np.float32)
    for b in range(B):
        bsel[b, :, b] = 1
        dmask[:, b, b] = 1
    put("bsel", bsel)
    put("dmask", dmask)
    put("ones", blocks(np.ones((32, 32), np.float32)))
    put("l1bias", np.tile(np.asarray(i["L1_conv_bias"]), B))
    put("win", blocks(np.asarray(i["L2_conv_W_in"]).T))
    put("bin", np.tile(np.asarray(i["L2_conv_b_in"]), B))
    qkv = np.stack([np.asarray(i["L2_conv_" + n])[0] for n in ("Wq", "Wk", "Wv")])
    put("qkv", qkv.transpose(3, 2, 0, 4, 1), 96)
    put("v2w", np.tile(np.asarray(i["L2_conv_Wv"])[2].reshape(32, C, 9).transpose(1, 2, 0), (B, 1, 1)))
    wproj = np.asarray(i["L2_conv_Wproj"])[list(GATES)]
    proj = np.zeros((HEADS, 32, 3, 32), np.float32)
    proj[:, 0:HC] = wproj[:, 0].reshape(3, 32, HEADS, HC).transpose(2, 3, 0, 1)
    put("proj", proj)
    put("proj2", np.tile(wproj[:, 2].transpose(2, 0, 1), (B, 1, 1)))
    put("gbias", np.tile(np.asarray(i["L2_conv_b_gates"])[list(GATES)].T, (B, 1)))
    put("wout", blocks(np.asarray(i["L2_conv_W_out"]).T))
    put("bout", np.tile(np.asarray(i["L2_conv_b_out"]), B))
    put("ident", np.eye(P, dtype=np.float32))
    m = transform_matrix(MODES)
    neg = -np.arange(MODES) % MODES
    put("mt", blocks(m.T))
    put("mrt", blocks(m[neg].T))
    put("mnt", blocks(m[:, neg].T))
    order = np.arange(MODES).reshape(4, 2, 4).transpose(1, 0, 2).reshape(-1)
    put("mt_back", blocks(m.T[order]))
    put("mnt_back", blocks(m[:, neg].T[order]))
    return c


def kernel(**inputs):
    import concourse.bacc as bacc
    from concourse.bass_utils import run_bass_kernel_spmd

    wmodes = np.asarray(inputs["L3_conv_weights1"]).reshape(C, 32, 4, KG // 2, 2, MODES)
    wmodes = wmodes.transpose(2, 0, 3, 5, 4, 1).reshape(P, KG * MODES * 32)
    arrays = {"x": np.ascontiguousarray(np.asarray(inputs["x"]).reshape(P, HW)),
              "consts": layout_consts(inputs), "wmodes": np.ascontiguousarray(wmodes)}
    nc = bacc.Bacc("TRN2", target_bir_lowering=False, num_devices=1)
    args = [nc.dram_tensor(n, a.shape, F32, kind="ExternalInput").ap() for n, a in arrays.items()]
    out = nc.dram_tensor("out", [P, HW], F32, kind="ExternalOutput").ap()
    build(nc, *args, out)
    r = run_bass_kernel_spmd(nc, [arrays], core_ids=[0])
    return r.results[0]["out"].reshape(B, C, H, W)
```

```python
from contextlib import ExitStack

import numpy as np

import concourse.bass as bass
from concourse import mybir

F32 = mybir.dt.float32
BF16 = mybir.dt.bfloat16
I32 = mybir.dt.int32
ACT = mybir.ActivationFunctionType
ALU = mybir.AluOpType
AX = mybir.AxisListType

P = 128
B, C, H, W = 4, 32, 32, 32
HW = H * W
HALF = HW // 2
WP = W + 2
NP = WP * WP
XPW = NP + 76
EPS = 1e-5

LINEAR = None
TILES = [
    ([(LINEAR, (0, 0)), ((0, 0), (0, 0)), ((0, 1), (0, 0)), ((1, 0), (0, 0))],
     [(py, px) for py in range(3) for px in range(3)]),
    ([((1, 1), (0, 0)), ((1, -1), (0, 1)), ((2, 0), (0, 0)), ((0, 2), (0, 0))],
     [(0, 0), (0, 1), (1, 0), (1, 1)]),
    ([((1, 2), (0, 0)), ((1, -2), (0, 2)), ((2, 0), (0, 2)), ((0, 2), (2, 0))], [(0, 0), (1, 0)]),
    ([((2, 1), (0, 0)), ((2, -1), (0, 1)), ((2, 2), (0, 0)), ((2, -2), (0, 2))], [(0, 0), (0, 1)]),
]
SLOTS_PER_TILE = P // C
N_MAPS = SLOTS_PER_TILE * len(TILES)
PLANE = 386
TOP = 18 * WP
CUTS = ((0, TOP), (TOP, NP))


def tap_pair(d, pre, py, px):
    dy, dx = d or (0, 0)
    py, px = py + pre[0], px + pre[1]
    qy, qx = py + dy, px + dx
    if max(py, px) > 2 or not (0 <= qy <= 2 and 0 <= qx <= 2):
        return None
    return py * 3 + px, qy * 3 + qx


SLOTS = [(t, offset) for t, (_, offsets) in enumerate(TILES) for offset in offsets]
N_KEPT = 45
_pairs = [(d is LINEAR, tap_pair(d, pre, *offset)) for maps, offsets in TILES for d, pre in maps
          for offset in offsets if tap_pair(d, pre, *offset)]
assert len(_pairs) == len(set(_pairs)) == 9 + N_KEPT
VOLTERRA_SCALE = float(np.float32(1.0 / np.sqrt(N_KEPT)))

HEADS, HC = 4, 8
G = B * HEADS
KH = H - 2
KEYS = KH * KH
KHALF = KEYS // 2
DT = KEYS // P
KREST = KEYS - DT * P
KPAD = DT * P + 32
KDIFF = KPAD
KW = KPAD + KHALF
K_RANGES = (slice(0, KPAD), slice(KDIFF, KW))
PARTS = 3
PAIR_ROWS = PARTS * PARTS * HC
S_ROWS = PAIR_ROWS + PARTS
HALF_TILES = HALF // P
ROWS_OF_MAX = HEADS * HALF_TILES
EXP_UNITS = HEADS * DT + 1
PRING = 8
TWO_ONES = float(np.array([0x3F803F80], np.uint32).view(np.float32)[0])
GATES = (0, 2, 3)
SCORE_RING = (0, 1, 2)
MAX_RING = (3, 4, 5)
O_RING = (6, 7)
PIECES = (slice(0, HALF), slice(HALF, HALF + HALF // 2), slice(HALF + HALF // 2, HW))
GATE_BANKS = ((3, 4, 5), (3, 4, 5), (0, 1, 2))
OUT_BANKS = (4, 7, 6)
MODES = 32
KG = MODES // 4

FIRST_AHEAD = 18
WIDE_AHEAD = 12
BLOCKS_PER_STEP = 4.15
MOVED = 4
MODE_STAGES = [(k2, lh) for k2 in range(2) for lh in range(2)]
POOL_MODES = 2


def attention_plan():
    stream, i = [], 0
    for s in range(2 * B):
        for a in range(ROWS_OF_MAX):
            pair = s < 2 or a % 8 in (0, 3, 6)
            for kind in (("diff", "first") if pair else ("first", "second")):
                stream.append(("max", i, s, a, kind))
                i += 1
        stream.append(("split", s))
        stream.append(("turn", i, s))
        i += 1
    for at in [at for at, item in enumerate(stream) if item[0] == "turn"]:
        n = min(MOVED, len(stream) - 1 - at)
        moved = stream[at + 1:at + 1 + n] + [stream[at]]
        numbers = sorted(item[1] for item in moved)
        stream[at:at + 1 + n] = [(item[0], k, *item[2:]) for item, k in zip(moved, numbers)]
    plan = []

    def take(n):
        while n > 0 and stream:
            item = stream.pop(0)
            plan.append(item)
            if item[0] != "split":
                n -= 1

    take(2 * ROWS_OF_MAX + 1 + FIRST_AHEAD)
    due, prev, later, step = 0.0, None, [], 0
    for s in range(2 * B):
        for t in range(DT + 1):
            units = HEADS if t < DT else 1
            due += BLOCKS_PER_STEP * (1.0 if t < DT else 0.6)
            taken = 0
            for h in range(units):
                plan.append(("score", s * EXP_UNITS + t * HEADS + h))
                k = int(due * (h + 1) / units + 1e-6)
                take(k - taken)
                taken = max(taken, k)
                if prev and h == min(2, units - 1):
                    plan.append(("values", *prev))
            due -= taken
            if prev and prev[1] == DT:
                later += [(step, ("read", prev[0])), (step + 1, ("write", prev[0]))]
                if prev[0] == 2 * B - 2:
                    later += [(step + 1, ("gates", 0)), (step + 2, ("cell", 0)), (step + 3, ("hidden", 0)),
                              (step + 4, ("out", 0))]
            plan += [item for at, item in later if at <= step]
            later = [(at, item) for at, item in later if at > step]
            prev = (s, t)
            step += 1
    plan += [("values", *prev)] + [item for _, item in later]
    plan += [("read", prev[0]), ("write", prev[0])]
    plan += [("gates", 1), ("cell", 1), ("gates", 2), ("hidden", 1), ("cell", 2), ("out", 1), ("hidden", 2),
             ("out", 2)]
    assert not stream
    return plan


CONSTS = {}


def _place(names):
    at = 0
    for name, n in names:
        CONSTS[name] = (at, n)
        at += n
    return at


N_FIRST = _place([("l0w", len(SLOTS) * 32), ("l0bias", 1)])
N_CONST = N_FIRST
for _name, _n in [("l1w", 3 * 32), ("bsel", 32), ("dmask", B), ("l1bias", 1), ("win", P), ("bin", 1), ("qkv", 3 * 3 * 32),
                  ("v2w", 9 * 32), ("proj", 3 * 32), ("proj2", 3 * 32), ("ones", P), ("gbias", 3), ("wout", P),
                  ("bout", 1), ("ident", P), ("mt", P), ("mrt", P), ("mnt", P), ("mt_back", P),
                  ("mnt_back", P)]:
    CONSTS[_name] = (N_CONST, _n)
    N_CONST += _n


def build(nc, x, consts, wmodes, out):
    ctx = ExitStack()
    with ctx:
        def sb(name, shape, dt=F32):
            return ctx.enter_context(nc.sbuf_tensor(name, shape, dt))

        def sem(name):
            return ctx.enter_context(nc.semaphore(name))

        xa = sb("xa", [P, HW])
        xb = sb("xb", [P, HW])
        xc = sb("xc", [P, HW])
        xp = sb("xp", [P, XPW])
        cst = sb("cst", [P, N_CONST])
        stats = sb("stats", [P, 12])
        small = sb("small", [P, 16])
        arena_a = sb("arena_a", [P, 8192 + G * KW // 2])
        arena_b = sb("arena_b", [P, PRING * HALF + B * HW + KG * MODES * C])
        vt = sb("vt", [P, DT, G, 32])
        vrest = sb("vrest", [P, B, P])
        ot = sb("ot", [P, 2, HALF])
        on = sb("on", [P, 2, HALF])
        rden = sb("rden", [P, 2, 16])
        relus = sb("relus", [P, 3, KHALF])
        sums = sb("sums", [P, 2, KHALF], BF16)
        mx = sb("mx", [P, ROWS_OF_MAX, 2])
        negm = sb("negm", [P, 2, ROWS_OF_MAX])
        mparts = sb("mparts", [P, PARTS, ROWS_OF_MAX], BF16)
        mt_sb = sb("mt_sb", [PARTS * ROWS_OF_MAX, P], BF16)
        ident_b = sb("ident_b", [P, P], BF16)
        wsum = sb("wsum", [P, 3, H])
        win9 = sb("win9", [P, 2, 9])
        a2 = sb("a2", [P, 1])
        gb = sb("gb", [P, 3])
        l1s = sb("l1s", [96, 3, P])
        zeros = sb("zeros", [P, 512], BF16)

        def c_(name, r0=0, r1=P):
            at, n = CONSTS[name]
            return cst[r0:r1, at:at + n]

        maps = arena_a[:, 0:N_MAPS * NP].rearrange("p (m n) -> p m n", n=NP)
        q_words = G * HW // 2
        k_words = G * KW // 2
        qst = arena_a[:, 0:q_words].bitcast(BF16).rearrange("p (e g n) -> p e g n", e=2, g=G)
        kst = arena_a[:, q_words:q_words + k_words].bitcast(BF16).rearrange("p (g n) -> p g n", g=G)
        xm = arena_a[:, 0:8192].rearrange("p (n m) -> p n m", m=64)
        tmp3 = arena_a[:, 8192:8192 + 6 * HW].rearrange("p (t n) -> p t n", n=HW)
        stack = arena_b[:, 0:3 * B * NP].rearrange("p (t b n) -> p t b n", t=3, b=B)
        xst = arena_b[:, 0:B * H * WP].rearrange("p (b n) -> p b n", b=B)
        at = B * H * WP
        q_res = arena_b[:, at:at + HW]
        k_res = arena_b[:, at + HW:at + HW + KW]
        at += HW + KW
        k_first = arena_b[:, at:at + KHALF]
        vs = arena_b[:, at + KHALF:at + KHALF + KEYS]
        assert at + KHALF + KEYS <= 8192
        q_parts = arena_b[:, 8192:8192 + PARTS * HW // 2].bitcast(BF16).rearrange("p (s n) -> p s n", s=PARTS)
        at = 8192 + PARTS * HW // 2
        k_parts = arena_b[:, at:at + PARTS * KW // 2].bitcast(BF16).rearrange("p (s n) -> p s n", s=PARTS)
        at += PARTS * KW // 2
        planes = arena_b[:, at:at + 3 * PLANE]
        assert at + 3 * PLANE <= 16384
        probs = arena_b[:, 0:PRING * HALF].rearrange("p (s n) -> p s n", n=HALF)
        attn = arena_b[:, PRING * HALF:PRING * HALF + B * HW].rearrange("p (b n) -> p b n", b=B)
        wm = arena_b[:, PRING * HALF + B * HW:]
        y1 = arena_b[:, 0:4 * HW]
        z1 = arena_b[:, 4 * HW:6 * HW]

        ps = ctx.enter_context(nc.psum_tensor("ps", [P, 8, 512], F32))

        def banks(i, n=2):
            return ps[:, i:i + n, :].rearrange("p a n -> p (a n)")

        q_dram = nc.dram_tensor("q_scratch", [PARTS, 2, HC, G, HALF], BF16, kind="Internal").ap()
        k_dram = nc.dram_tensor("k_scratch", [PARTS, HC, G, KW], BF16, kind="Internal").ap()

        x_loaded = [sem("x_loaded0"), sem("x_loaded1")]
        first_loaded = sem("first_loaded")
        consts_loaded = sem("consts_loaded")
        wm_loaded = sem("wm_loaded")
        dve_step = sem("dve_step")
        padded = sem("padded")
        zeros_ready = sem("zeros_ready")
        xp_zeroed = sem("xp_zeroed")
        act_map = sem("act_map")
        map_ready = sem("map_ready")
        tile0_top = sem("tile0_top")
        tile_in = [sem(f"tile_in{t}") for t in range(len(TILES))]
        l0_done = sem("l0_done")
        l0_read = sem("l0_read")
        l1s_done = sem("l1s_done")
        l1s_ready = sem("l1s_ready")
        planes_done = sem("planes_done")
        planes_ready = sem("planes_ready")
        l1_done = sem("l1_done")
        l1_read = sem("l1_read")
        xst_zeroed = sem("xst_zeroed")
        xin_done = sem("xin_done")
        xin_act = sem("xin_act")
        xin_dve = sem("xin_dve")
        xin_ready = sem("xin_ready")
        k_zeroed = sem("k_zeroed")
        q_done = sem("q_done")
        k_done = sem("k_done")
        v_done = sem("v_done")
        k_copied = sem("k_copied")
        k_part = [sem(f"k_part{s}") for s in range(PARTS)]
        q_part = [sem(f"q_part{s}") for s in range(PARTS)]
        vs_ready = sem("vs_ready")
        vt_done = sem("vt_done")
        vt_ready = sem("vt_ready")
        vt_zeroed = sem("vt_zeroed")
        win_ready = sem("win_ready")
        win_done = sem("win_done")
        win_scaled = sem("win_scaled")
        a2_done = sem("a2_done")
        a2_ready = sem("a2_ready")
        gb_done = sem("gb_done")
        gb_ready = sem("gb_ready")
        qd_written = [sem("qd_written0"), sem("qd_written1")]
        kd_written = sem("kd_written")
        q_filled = sem("q_filled")
        k_filled = sem("k_filled")
        k_padded = sem("k_padded")
        tile0_used = sem("tile0_used")
        q_in = [sem(f"q_in{i}") for i in range(3)]
        k_in = [sem(f"k_in{i}") for i in range(3)]
        max_scored = sem("max_scored")
        max_read = sem("max_read")
        max_relu = sem("max_relu")
        m_split = sem("m_split")
        m_in = sem("m_in")
        scored = sem("scored")
        expd = sem("expd")
        pv_done = sem("pv_done")
        o_read = sem("o_read")
        o_summed = sem("o_summed")
        o_scaled = sem("o_scaled")
        attn_ready = sem("attn_ready")
        gate_done = sem("gate_done")
        gate_act = sem("gate_act")
        cell_ready = sem("cell_ready")
        cell_act = sem("cell_act")
        h_ready = sem("h_ready")
        wout_done = sem("wout_done")
        x3_ready = sem("x3_ready")
        xm_zeroed = sem("xm_zeroed")
        t1_ready = sem("t1_ready")
        rows_done = sem("rows_done")
        t2_ready = sem("t2_ready")
        cols_done = sem("cols_done")
        tu_ready = sem("tu_ready")
        xm_dve = sem("xm_dve")
        xm_pool = sem("xm_pool")
        mix_done = sem("mix_done")
        y1_ready = sem("y1_ready")
        inv_l_done = sem("inv_l_done")
        z1_ready = sem("z1_ready")
        inv_k_done = sem("inv_k_done")
        res_ready = sem("res_ready")
        stored = sem("stored")

        block = ctx.enter_context(nc.Block())

        def interior(ap):
            return ap[:, WP + 1:WP + 1 + 32 * WP].rearrange("p (y x) -> p y x", x=WP)[:, :, 0:W]

        def window(image, py, px, y0, ny, nx):
            rows = image[:, (y0 + py) * WP:(y0 + py + ny) * WP].rearrange("p (y x) -> p y x", x=WP)
            return rows[:, :, px:px + nx]

        plan = attention_plan()
        prologue = 2 * ROWS_OF_MAX + WIDE_AHEAD

        def block_bank(i):
            ring = SCORE_RING + MAX_RING if i < prologue else MAX_RING
            return ring[i % len(ring)]

        def block_before(i, bank):
            return max((j for j in range(max(0, i - 14), i) if block_bank(j) == bank), default=None)

        blocks_read = {}
        diffs = []
        split_after = {}
        vector_reads = 0
        for item in plan:
            if item[0] == "split":
                split_after[item[1]] = vector_reads
            elif item[0] == "turn" or (item[0] == "max" and item[4] != "diff"):
                vector_reads += 1
                blocks_read[item[1]] = (max_read, vector_reads)
            elif item[0] == "max":
                diffs.append(item[1])
                blocks_read[item[1]] = (max_relu, len(diffs))
        turn_of = {item[2]: item[1] for item in plan if item[0] == "turn"}

        def piece_bank(bank, p):
            return ps[:, bank, 0:PIECES[p].stop - PIECES[p].start]

        def first_of_pair(i):
            return i + 1

        def mode_part(engine, k2, lh, g, part):
            rows = slice(32 * g, 32 * g + 32)
            half = slice(lh * MODES, (lh + 1) * MODES)
            dst = xm[rows].rearrange("p (jh k l) (jl m) -> p jh k (l jl) m", jh=2, k=2, jl=2)[
                :, :, k2, half, 8 * g + 4 * part:8 * g + 4 * part + 4]
            v = tmp3[rows, 4, :].rearrange("p (jh k n b) -> p jh k n b", jh=2, k=2, b=B)[:, :, k2, half]
            u = tmp3[rows, 3, :].rearrange("p (jh k n b) -> p jh k n b", jh=2, k=2, b=B)[:, :, k2, half]
            return engine.tensor_tensor(dst, v, u, ALU.subtract if part else ALU.add)

        def xin_bank(n):
            return ps[0:96, (2 + n) % 8, :].rearrange("p (y x) -> p y x", x=W)

        def xin_slot(n):
            e, b = divmod(n, B)
            return xst[0:96, b, 16 * e * WP:16 * (e + 1) * WP].rearrange("p (y x) -> p y x", x=WP)[:, :, 1:1 + W]

        GN_STEPS = 3 + 3 + 6
        K_DIFF = 3 * GN_STEPS + 1
        K_RESID = (K_DIFF + 1, K_DIFF + 2)
        Q_RESID = (K_DIFF + 3, K_DIFF + 4)

        @block.sync
        def _(sp):
            for e in range(2):
                half = slice(e * HALF, (e + 1) * HALF)
                sp.dma_start(xa[:, half], x[:, half]).then_inc(x_loaded[e], 16)
            sp.dma_start(cst[:, 0:N_FIRST], consts[:, 0:N_FIRST]).then_inc(first_loaded, 16)
            def stack_tile(t, n0, n1, signal):
                maps_ = slice(SLOTS_PER_TILE * t, SLOTS_PER_TILE * (t + 1))
                for b in range(B):
                    sp.dma_start(stack[:, t % 3, b, n0:n1], maps[32 * b:32 * b + 32, maps_, n0:n1]
                                 ).then_inc(signal, 16)

            for cut, signal in enumerate((tile0_top, tile_in[0])):
                sp.wait_ge(act_map, 2 * cut + 2)
                sp.wait_ge(map_ready, 2 * cut + 2)
                stack_tile(0, *CUTS[cut], signal)
            for t in range(1, len(TILES)):
                sp.wait_ge(map_ready, SLOTS_PER_TILE * (t + 1))
                if t == 3:
                    sp.wait_ge(tile0_used, 1)
                stack_tile(t, 0, NP, tile_in[t])
            sp.dma_start(cst[:, N_FIRST:N_CONST], consts[:, N_FIRST:N_CONST]).then_inc(consts_loaded, 16)
            for s in range(PARTS):
                sp.wait_ge(k_part[s], 2)
                if s == 0:
                    sp.wait_ge(k_zeroed, 2)
                sp.dma_start(k_dram[s].rearrange("c g n -> g c n"), k_parts[:, s, :]).then_inc(kd_written, 16)
            for s in range(PARTS):
                sp.wait_ge(q_part[s], 1)
                sp.dma_start(q_dram[s, 0].rearrange("c g n -> g c n"), q_parts[:, s, 0:HALF]
                             ).then_inc(qd_written[0], 16)

            def stack_k(i, g0, g1):
                src = k_dram[:, :, g0:g1, :].rearrange("t c g n -> (t c) (g n)")
                sp.dma_start(kst[0:PAIR_ROWS, g0:g1, :].rearrange("p g n -> p (g n)"),
                             src.unsqueeze(0).to_broadcast([PARTS, PARTS * HC, (g1 - g0) * KW])
                             ).then_inc(k_in[i], 16)

            def stack_q(i, e, g0, g1):
                for s in range(PARTS):
                    r0 = s * PARTS * HC
                    src = q_dram[s, e, :, g0:g1, :].rearrange("c g n -> c (g n)")
                    sp.dma_start(qst[r0:r0 + PARTS * HC, e, g0:g1, :].rearrange("p g n -> p (g n)"),
                                 src.unsqueeze(0).to_broadcast([PARTS, HC, (g1 - g0) * HALF])
                                 ).then_inc(q_in[i], 16)

            sp.wait_ge(k_padded, 1)
            sp.wait_ge(q_filled, 1)
            sp.wait_ge(kd_written, PARTS * 16)
            stack_k(0, 0, HEADS // 2)
            sp.wait_ge(qd_written[0], PARTS * 16)
            stack_q(0, 0, 0, HEADS)
            stack_k(1, HEADS // 2, HEADS)
            stack_q(1, 0, HEADS, G)
            stack_k(2, HEADS, G)
            for s in range(PARTS):
                sp.wait_ge(q_part[s], 2)
                sp.dma_start(q_dram[s, 1].rearrange("c g n -> g c n"), q_parts[:, s, HALF:HW]
                             ).then_inc(qd_written[1], 16)
            for s in range(2 * B):
                e, b = divmod(s, B)
                sp.wait_ge(*blocks_read[turn_of[s]])
                sp.dma_start(qst[PAIR_ROWS:S_ROWS, e, b * HEADS:(b + 1) * HEADS, :].rearrange("p g n -> p (g n)"),
                             mt_sb[:]).then_inc(m_in, 16)
                if s == 0:
                    sp.wait_ge(qd_written[1], PARTS * 16)
                    stack_q(2, 1, 0, G)
                    sp.dma_start(wm, wmodes).then_inc(wm_loaded, 16)
            for e in range(2):
                half = slice(e * HALF, (e + 1) * HALF)
                sp.wait_ge(res_ready, e + 1)
                sp.dma_start(out[:, half], xb[:, half]).then_inc(stored, 16)
            sp.wait_ge(stored, 2 * 16)

        @block.gpsimd
        def _(pool):
            nc.gpsimd.memset(zeros[:], 0.0).then_inc(zeros_ready, 1)
            nc.gpsimd.memset(xp[:], 0.0).then_inc(xp_zeroed, 1)
            nc.gpsimd.memset(vt[:], 0.0).then_inc(vt_zeroed, 1)
            nc.gpsimd.memset(vrest[:], 0.0).then_inc(vt_zeroed, 1)
            pool.wait_ge(vt_zeroed, 2)
            pool.wait_ge(tile0_top, B * 16)
            for t in range(2):
                pool.wait_ge(tile_in[t], B * 16)
            nc.gpsimd.memset(arena_a[64:P, 0:q_words], 0.0).then_inc(q_filled, 1)
            pool.wait_ge(q_filled, 1)
            pool.wait_ge(l0_done, 1)
            nc.gpsimd.memset(xst[:], 0.0).then_inc(xst_zeroed, 1)
            pool.wait_ge(xst_zeroed, 1)
            pool.wait_ge(k_filled, 2)
            nc.gpsimd.memset(kst[64:P, :, KEYS:KPAD], 0.0).then_inc(k_padded, 1)
            pool.wait_ge(k_padded, 1)
            pool.wait_ge(l0_read, 2)
            nc.gpsimd.memset(k_parts[:, 0, KEYS:KPAD], 0.0).then_inc(k_zeroed, 1)
            nc.gpsimd.memset(k_res[:, KEYS:KPAD], 0.0).then_inc(k_zeroed, 1)
            pool.wait_ge(k_zeroed, 2)
            pool.wait_ge(xin_act, 2)
            pool.wait_ge(xin_dve, 2)
            nc.gpsimd.memset(xst[0:32, :, 0:WP], 0.0).then_inc(xin_ready, 1)
            pool.wait_ge(xin_act, 4)
            pool.wait_ge(xin_dve, 4)
            pool.wait_ge(xin_ready, 1)
            nc.gpsimd.memset(xst[64:96, :, (H - 1) * WP:H * WP], 0.0).then_inc(xin_ready, 1)
            pool.wait_ge(vt_ready, 2 + HEADS)
            pool.wait_ge(xin_ready, 2)
            nc.gpsimd.memset(vt[:, :, :, HC:HC + 1], 1.0).then_inc(vt_zeroed, 1)
            for h in range(HEADS):
                pool.wait_ge(vt_zeroed, 3 + h)
                nc.gpsimd.memset(vrest[32 * h:32 * h + KREST, :, 32 * h + HC:32 * h + HC + 1], 1.0
                                 ).then_inc(vt_zeroed, 1)
            for n in range(2 * B - 1):
                pool.wait_ge(o_summed, n + 1)
                if n >= 2:
                    pool.wait_ge(attn_ready, n - 1)
                nc.gpsimd.tensor_tensor(on[:, n % 2, :].rearrange("p (a c) -> p a c", c=32),
                                        ot[:, n % 2, :].rearrange("p (a c) -> p a c", c=32),
                                        rden[:, n % 2, :, None].to_broadcast([P, 16, 32]),
                                        ALU.mult).then_inc(o_scaled, 1)
            pool.wait_ge(scored, 2 * B * EXP_UNITS)
            nc.gpsimd.memset(arena_a[:, 0:8192], 0.0).then_inc(xm_zeroed, 1)
            pool.wait_ge(tu_ready, 8)
            pool.wait_ge(xm_zeroed, 1)
            for i, stage in enumerate(MODE_STAGES):
                for g in range(POOL_MODES):
                    if i or g:
                        pool.wait_ge(xm_pool, i * POOL_MODES + g)
                    mode_part(nc.gpsimd, *stage, g, 1).then_inc(xm_pool, 1)

        @block.scalar
        def _(act):
            act.wait_ge(padded, 1)
            for n0, n1 in CUTS:
                nc.scalar.activation(maps[:, 0, n0:n1], xp[:, n0:n1], ACT.Copy).then_inc(act_map, 1)
                nc.scalar.activation(maps[:, 1, n0:n1], xp[:, n0:n1], ACT.Square, scale=VOLTERRA_SCALE ** 0.5
                                     ).then_inc(act_map, 1)
            act.wait_ge(l0_done, 1)
            for i in range(3):
                act.wait_ge(planes_done, i + 1)
                nc.scalar.activation(planes[0:96, i * PLANE:(i + 1) * PLANE], ps[0:96, 2 + i, 0:PLANE], ACT.Copy
                                     ).then_inc(planes_ready, 1)
            act.wait_ge(consts_loaded, 16)
            act.wait_ge(xst_zeroed, 1)
            for n in range(0, 2 * B, 2):
                act.wait_ge(xin_done, n + 1)
                nc.scalar.activation(xin_slot(n), xin_bank(n), ACT.Identity, bias=c_("bin", 0, 96)
                                     ).then_inc(xin_act, 1)
            act.wait_ge(k_done, 2)
            nc.scalar.activation(k_first, ps[:, 2, 0:KHALF], ACT.Copy).then_inc(k_copied, 1)
            nc.scalar.activation(k_parts[:, 0, 0:KEYS].rearrange("p (a n) -> p a n", a=2),
                                 ps[:, 2:4, 0:KHALF], ACT.Copy).then_inc(k_part[0], 1)
            act.wait_ge(dve_step, K_DIFF)
            nc.scalar.activation(k_parts[:, 0, KDIFF:KW], k_res[:, KDIFF:KW], ACT.Copy).then_inc(k_part[0], 1)
            act.wait_ge(k_zeroed, 2)
            for i, cols in enumerate(K_RANGES):
                act.wait_ge(dve_step, K_RESID[i])
                nc.scalar.activation(k_parts[:, 1, cols], k_res[:, cols], ACT.Copy).then_inc(k_part[1], 1)
            for e in range(2):
                half = slice(e * HALF, (e + 1) * HALF)
                act.wait_ge(q_done, e + 1)
                nc.scalar.activation(q_parts[:, 0, half], ps[:, 4 + e, :], ACT.Copy).then_inc(q_part[0], 1)
                act.wait_ge(dve_step, Q_RESID[e])
                nc.scalar.activation(q_parts[:, 1, half], q_res[:, half], ACT.Copy).then_inc(q_part[1], 1)
            act.wait_ge(v_done, 2)
            nc.scalar.activation(vs.rearrange("p (a n) -> p a n", a=2), ps[:, 6:8, 0:KHALF],
                                 ACT.Copy).then_inc(vs_ready, 1)
            for item in plan:
                if item[0] == "score":
                    n = item[1]
                    act.wait_ge(scored, n + 1)
                    if n >= PRING:
                        old_half, old = divmod(n - PRING, EXP_UNITS)
                        act.wait_ge(pv_done, old_half * (DT + 1) + old // HEADS + 1)
                    nc.scalar.activation(probs[:, n % PRING, :], ps[:, SCORE_RING[n % len(SCORE_RING)], :], ACT.Exp).then_inc(expd, 1)
                elif item[0] == "max" and item[4] == "diff":
                    i = item[1]
                    d = diffs.index(i)
                    act.wait_ge(max_scored, i + 1)
                    if d >= 3:
                        act.wait_ge(*blocks_read[first_of_pair(diffs[d - 3])])
                    nc.scalar.activation(relus[:, d % 3, :], ps[:, block_bank(i), 0:KHALF], ACT.Relu
                                         ).then_inc(max_relu, 1)
                elif item[0] == "gates":
                    p = item[1]
                    act.wait_ge(gb_ready, 1)
                    for i in range(3):
                        act.wait_ge(gate_done, 3 * p + i + 1)
                        nc.scalar.activation(tmp3[:, i, PIECES[p]], piece_bank(GATE_BANKS[p][i], p), ACT.Tanh,
                                             bias=gb[:, i:i + 1], scale=1.0 if i == 1 else 0.5).then_inc(gate_act, 1)
                elif item[0] == "cell":
                    p = item[1]
                    act.wait_ge(cell_ready, p + 1)
                    nc.scalar.activation(tmp3[:, 4, PIECES[p]], tmp3[:, 3, PIECES[p]], ACT.Tanh, scale=0.5
                                         ).then_inc(cell_act, 1)

        @block.vector
        def _(dve):
            chain = [0]

            def link(ins):
                chain[0] += 1
                ins.then_inc(dve_step, 1)
                dve.wait_ge(dve_step, chain[0])

            def norm(src, dst):
                link(nc.vector.bn_stats(stats[:, 0:6], src[:, 0:HALF]))
                link(nc.vector.bn_stats(stats[:, 6:12], src[:, HALF:HW]))
                return norm_from_stats(src, dst)

            def norm_from_stats(src, dst):
                link(nc.vector.bn_aggr(small[:, 0:2], stats[:, :].rearrange("p (a b) -> p a b", b=6)))
                mean, var, v, y, t, nh = (small[:, i:i + 1] for i in range(6))
                nc.vector.tensor_scalar(nh, var, EPS, -0.5, ALU.add, ALU.mult).then_inc(dve_step, 1)
                chain[0] += 1
                link(nc.vector.tensor_scalar(v, var, EPS, None, ALU.add))
                link(nc.vector.tensor_scalar(y.bitcast(I32), v.bitcast(I32), -0.5, float(0x5F3759DF),
                                             ALU.mult, ALU.add))
                for _ in range(3):
                    link(nc.vector.scalar_tensor_tensor(t, y, nh, y, ALU.mult, ALU.mult))
                    link(nc.vector.scalar_tensor_tensor(y, t, 1.5, y, ALU.add, ALU.mult))
                return nc.vector.tensor_scalar(dst, src3(src, dst), mean, y, ALU.subtract, ALU.mult)

            def src3(src, dst):
                return src.rearrange("p (y x) -> p y x", x=W) if len(dst.shape) == 3 else src

            for e in range(2):
                dve.wait_ge(x_loaded[e], 16)
                link(nc.vector.bn_stats(stats[:, 6 * e:6 * e + 6], xa[:, e * HALF:(e + 1) * HALF]))
            dve.wait_ge(xp_zeroed, 1)
            norm_from_stats(xa[:], interior(xp)).then_inc(padded, 1)
            dve.wait_ge(padded, 1)
            order = [(SLOTS_PER_TILE * t + i, d, sy * WP + sx) for t, (maps_, _) in enumerate(TILES)
                     for i, (d, (sy, sx)) in enumerate(maps_)]
            steps = [(n0, n1, *step) for n0, n1 in CUTS for step in order[2:4]]
            steps += [(0, NP, *step) for step in order[4:]]
            for n0, n1, m, (dy, dx), pre in steps:
                at = dy * WP + dx + pre
                nc.vector.scalar_tensor_tensor(maps[:, m, n0:n1], xp[:, pre + n0:pre + n1], VOLTERRA_SCALE,
                                               xp[:, at + n0:at + n1], ALU.mult, ALU.mult).then_inc(map_ready, 1)
            dve.wait_ge(tile0_top, B * 16)
            last_tile = (N_MAPS - 4) * NP
            for t, (w0, w1) in ((2, (q_words, last_tile)), (3, (last_tile, q_words + k_words))):
                for tile in range(t + 1):
                    dve.wait_ge(tile_in[tile], B * 16)
                nc.vector.memset(arena_a[64:P, w0:w1], TWO_ONES).then_inc(k_filled, 1)
            dve.wait_ge(l0_done, 1)
            dve.wait_ge(first_loaded, 16)
            l0t = stack[:, 2, 0, 0:HW]
            nc.vector.transpose(l0t.rearrange("p (j o) -> p j o", o=32),
                                banks(0).rearrange("p (i j) -> p j i", j=32)).then_inc(l0_read, 1)
            dve.wait_ge(l0_read, 1)
            nc.vector.scalar_tensor_tensor(xb[:], l0t, c_("l0bias"), xa[:], ALU.add, ALU.add).then_inc(l0_read, 1)
            dve.wait_ge(l0_read, 2)
            dve.wait_ge(act_map, 4)
            norm(xb[:], interior(xp)).then_inc(padded, 1)
            dve.wait_ge(consts_loaded, 16)
            dve.wait_ge(l1s_done, 1)
            for px in range(3):
                nc.vector.tensor_tensor(
                    l1s[:, px, :].rearrange("p (b o) -> p b o", b=B),
                    ps[0:96, 7, px * 32:(px + 1) * 32].unsqueeze(1).to_broadcast([96, B, 32]),
                    c_("dmask", 0, 96).unsqueeze(2).to_broadcast([96, B, 32]), ALU.mult).then_inc(l1s_ready, 1)
            for e in range(2):
                half = slice(e * HALF, (e + 1) * HALF)
                dve.wait_ge(l1_done, e + 1)
                nc.vector.scalar_tensor_tensor(xc[:, half], ps[:, e, :], c_("l1bias"), xb[:, half], ALU.add, ALU.add
                                               ).then_inc(l1_read, 1)
                dve.wait_ge(l1_read, e + 1)
                link(nc.vector.bn_stats(stats[:, 6 * e:6 * e + 6], xc[:, half]))
            dve.wait_ge(planes_done, 3)
            norm_from_stats(xc[:], interior(xp)).then_inc(padded, 1)
            dve.wait_ge(padded, 3)
            dve.wait_ge(xst_zeroed, 1)
            for n in range(1, 2 * B, 2):
                dve.wait_ge(xin_done, n + 1)
                nc.vector.tensor_scalar(xin_slot(n), xin_bank(n), c_("bin", 0, 96), None, ALU.add
                                        ).then_inc(xin_dve, 1)
            nc.vector.tensor_scalar(xb[:], xc[:], c_("bout"), None, ALU.add).then_inc(l1_read, 1)
            nc.vector.tensor_copy(ident_b[:], c_("ident")).then_inc(l1_read, 1)
            nc.vector.memset(mx[:], -3.0e38).then_inc(l1_read, 1)
            rows = xp[:, WP:WP + 32 * WP].rearrange("p (y x) -> p y x", x=WP)
            for v in range(3):
                nc.vector.tensor_reduce(wsum[:, v, :], rows[:, :, 1 + v:1 + v + KH], AX.X, ALU.add
                                        ).then_inc(win_ready, 1)
            dve.wait_ge(win_ready, 3)
            for u in range(3):
                nc.vector.tensor_reduce(win9[:, 0, 3 * u:3 * u + 3], wsum[:, :, u:u + KH], AX.X, ALU.add
                                        ).then_inc(win_ready, 1)
            dve.wait_ge(k_copied, 1)
            dve.wait_ge(k_part[0], 1)
            link(nc.vector.tensor_tensor(k_res[:, KDIFF:KW], ps[:, 3, 0:KHALF], k_first, ALU.subtract))
            assert chain[0] == K_DIFF
            link(nc.vector.tensor_tensor(k_res[:, 0:KEYS].rearrange("p (a n) -> p a n", a=2),
                                         ps[:, 2:4, 0:KHALF],
                                         k_parts[:, 0, 0:KEYS].rearrange("p (a n) -> p a n", a=2),
                                         ALU.subtract))
            dve.wait_ge(k_part[0], 2)
            link(nc.vector.tensor_tensor(k_res[:, KDIFF:KW], k_res[:, KDIFF:KW], k_parts[:, 0, KDIFF:KW],
                                         ALU.subtract))
            assert chain[0] == K_RESID[1]
            dve.wait_ge(win_done, 1)
            nc.vector.tensor_scalar(win9[:, 1, :], ps[:, 0, 16:25], 1.0 / KEYS, c_("bin"), ALU.mult, ALU.add
                                    ).then_inc(win_scaled, 1)
            dve.wait_ge(k_zeroed, 2)
            for i, cols in enumerate(K_RANGES):
                dve.wait_ge(k_part[1], i + 1)
                nc.vector.tensor_tensor(k_parts[:, 2, cols], k_res[:, cols], k_parts[:, 1, cols], ALU.subtract
                                        ).then_inc(k_part[2], 1)
            for e in range(2):
                half = slice(e * HALF, (e + 1) * HALF)
                dve.wait_ge(q_part[0], e + 1)
                link(nc.vector.tensor_tensor(q_res[:, half], ps[:, 4 + e, :], q_parts[:, 0, half], ALU.subtract))
                assert chain[0] == Q_RESID[e]
                if e == 1:
                    dve.wait_ge(a2_done, 1)
                    nc.vector.tensor_copy(a2[:], ps[:, 0, 0:1]).then_inc(a2_ready, 1)
                dve.wait_ge(q_part[1], e + 1)
                nc.vector.tensor_tensor(q_parts[:, 2, half], q_res[:, half], q_parts[:, 1, half], ALU.subtract
                                        ).then_inc(q_part[2], 1)
            dve.wait_ge(gb_done, 1)
            link(nc.vector.tensor_tensor(gb[:], ps[:, 0, 8:11], c_("gbias"), ALU.add))
            for i in (0, 2):
                nc.vector.tensor_scalar(gb[:, i:i + 1], gb[:, i:i + 1], 0.5, None, ALU.mult).then_inc(gb_ready, 1)
            dve.wait_ge(vt_zeroed, 2)
            dve.wait_ge(vt_done, 1)
            nc.vector.tensor_copy(vt[:, 0:4, :, 0:HC],
                                  ps[:, 0, :].rearrange("p (t g c) -> p t g c", t=4, c=HC)).then_inc(vt_ready, 1)
            dve.wait_ge(vt_done, 2)
            nc.vector.tensor_copy(vt[:, 4:DT, :, 0:HC],
                                  ps[:, 1, 0:(DT - 4) * P].rearrange("p (t g c) -> p t g c", t=DT - 4, c=HC)
                                  ).then_inc(vt_ready, 1)
            for h in range(HEADS):
                r = slice(32 * h, 32 * h + KREST)
                nc.vector.tensor_copy(vrest[r, :, 32 * h:32 * h + HC],
                                      ps[r, 1, 3 * P:4 * P].rearrange("p (b h c) -> p b h c", h=HEADS, c=HC)[:, :, h, :]
                                      ).then_inc(vt_ready, 1)

            def split_max(s):
                dve.wait_ge(max_read, split_after[s])
                link(nc.vector.tensor_reduce(negm[:, 0, :], mx[:], AX.X, ALU.max, negate=True))
                if s > 0:
                    dve.wait_ge(max_scored, turn_of[s - 1] + 1)
                link(nc.vector.tensor_copy(mparts[:, 0, :], negm[:, 0, :]))
                link(nc.vector.tensor_tensor(negm[:, 1, :], negm[:, 0, :], mparts[:, 0, :], ALU.subtract))
                link(nc.vector.tensor_copy(mparts[:, 1, :], negm[:, 1, :]))
                nc.vector.tensor_tensor(mparts[:, 2, :], negm[:, 1, :], mparts[:, 1, :], ALU.subtract
                                        ).then_inc(m_split, 1)

            dve.wait_ge(l1_read, 5)
            for item in plan:
                if item[0] == "max" and item[4] != "diff":
                    _, i, _, a, kind = item
                    dve.wait_ge(max_scored, i + 1)
                    bank = ps[:, block_bank(i), 0:KHALF]
                    if i - 1 in diffs:
                        d = diffs.index(i - 1)
                        dve.wait_ge(max_relu, d + 1)
                        if d >= 2:
                            dve.wait_ge(*blocks_read[first_of_pair(diffs[d - 2])])
                        nc.vector.tensor_tensor_reduce(out=sums[:, d % 2, :], in0=bank, in1=relus[:, d % 3, :],
                                                       scale=1.0, scalar=-3.0e38, op0=ALU.add, op1=ALU.max,
                                                       accum_out=mx[:, a, 0:1]).then_inc(max_read, 1)
                    else:
                        e = 0 if kind == "first" else 1
                        nc.vector.tensor_reduce(mx[:, a, e:e + 1], bank, AX.X, ALU.max).then_inc(max_read, 1)
                elif item[0] == "split":
                    split_max(item[1])
                elif item[0] == "turn":
                    _, i, s = item
                    dve.wait_ge(max_scored, i + 1)
                    if s > 0:
                        dve.wait_ge(m_in, 16 * s)
                    nc.vector.tensor_copy(mt_sb[:], ps[0:PARTS * ROWS_OF_MAX, block_bank(i), 0:P // 2].bitcast(BF16)
                                          ).then_inc(max_read, 1)
                elif item[0] == "read":
                    n = item[1]
                    dve.wait_ge(pv_done, (n + 1) * (DT + 1))
                    if n >= 2:
                        dve.wait_ge(o_scaled, n - 1)
                    nc.vector.transpose(ot[:, n % 2, :], ps[:, O_RING[n % len(O_RING)], :]).then_inc(o_read, 1)
                    dve.wait_ge(o_read, n + 1)
                    nc.vector.reciprocal(rden[:, n % 2, :, None],
                                         ot[:, n % 2, :].rearrange("p (a c) -> p a c", c=32)[:, :, HC:HC + 1]
                                         ).then_inc(o_summed, 1)
                elif item[0] == "write":
                    n = item[1]
                    if n == 2 * B - 1:
                        dve.wait_ge(o_summed, n + 1)
                        link(nc.vector.tensor_tensor(on[:, n % 2, :].rearrange("p (a c) -> p a c", c=32),
                                                     ot[:, n % 2, :].rearrange("p (a c) -> p a c", c=32),
                                                     rden[:, n % 2, :, None].to_broadcast([P, 16, 32]), ALU.mult))
                    else:
                        dve.wait_ge(o_scaled, n + 1)
                    e, b = divmod(n, B)
                    nc.vector.transpose(attn[:, b, e * HALF:(e + 1) * HALF], on[:, n % 2, :]
                                        ).then_inc(attn_ready, 1)
                elif item[0] == "cell":
                    p = item[1]
                    dve.wait_ge(gate_act, 3 * p + 2)
                    nc.vector.scalar_tensor_tensor(tmp3[:, 3, PIECES[p]], tmp3[:, 0, PIECES[p]], 1.0,
                                                   tmp3[:, 1, PIECES[p]], ALU.add, ALU.mult).then_inc(cell_ready, 1)
                elif item[0] == "hidden":
                    p = item[1]
                    dve.wait_ge(gate_act, 3 * p + 3)
                    dve.wait_ge(cell_act, p + 1)
                    nc.vector.scalar_tensor_tensor(tmp3[:, 5, PIECES[p]], tmp3[:, 2, PIECES[p]], 1.0,
                                                   tmp3[:, 4, PIECES[p]], ALU.add, ALU.mult).then_inc(h_ready, 1)
                elif item[0] == "out":
                    p = item[1]
                    dve.wait_ge(wout_done, p + 1)
                    nc.vector.scalar_tensor_tensor(xc[:, PIECES[p]], piece_bank(OUT_BANKS[p], p), 0.5, xb[:, PIECES[p]],
                                                   ALU.mult, ALU.add).then_inc(x3_ready, 1)
                    if p != 1:
                        e = min(p, 1)
                        dve.wait_ge(x3_ready, p + 1)
                        link(nc.vector.bn_stats(stats[:, 6 * e:6 * e + 6], xc[:, e * HALF:(e + 1) * HALF]))
            link(norm_from_stats(xc[:], xa[:]))
            for e in range(2):
                nc.vector.transpose(tmp3[:, 0, e * HALF:(e + 1) * HALF].rearrange("p (w c) -> p w c", c=C),
                                    xa[:, :].rearrange("p (h w) -> p w h", w=W)[:, e * W // 2:(e + 1) * W // 2]
                                    ).then_inc(t1_ready, 1)
            for i in range(2):
                dve.wait_ge(rows_done, i + 1)
                nc.vector.transpose(tmp3[:, 1 + i, :].rearrange("p (c k) -> p c k", k=MODES),
                                    banks(2 * i).rearrange("p (w c) -> p c w", c=C)).then_inc(t2_ready, 1)
            for i in range(2):
                src = banks(4 + 2 * i).rearrange("p (b c k jl) -> p b k jl c", b=B, c=C, jl=2)
                dst = tmp3[:, 3 + i, :].rearrange("p (k l jl b) -> p b k jl l", b=B, l=MODES, jl=2)
                for b in range(B):
                    if b % 2 == 0:
                        dve.wait_ge(cols_done, 2 * i + b // 2 + 1)
                    nc.vector.transpose(dst[:, b], src[:, b]).then_inc(tu_ready, 1)
            dve.wait_ge(tu_ready, 8)
            dve.wait_ge(xm_zeroed, 1)
            for stage in MODE_STAGES:
                for g in range(4):
                    mode_part(nc.vector, *stage, g, 0).then_inc(xm_dve, 1)
                    if g >= POOL_MODES:
                        mode_part(nc.vector, *stage, g, 1).then_inc(xm_dve, 1)
            for k2 in range(2):
                dve.wait_ge(mix_done, k2 + 1)
                for jl in range(2):
                    nc.vector.transpose(
                        y1[:, (2 * k2 + jl) * HW:(2 * k2 + jl + 1) * HW].rearrange("p (o m) -> p o m", m=32),
                        banks(4 * k2, 4).rearrange("p (l j o) -> p j o l", j=2, o=C)[:, jl]).then_inc(y1_ready, 1)
            for s in range(2):
                dve.wait_ge(inv_l_done, s + 1)
                nc.vector.transpose(z1[:, s * HW:(s + 1) * HW].rearrange("p (o h l) -> p o h l", h=2, l=16),
                                    ps[:, 2 * s:2 * s + 2, :].rearrange("p h (o k) -> p o h k", o=C)
                                    ).then_inc(z1_ready, 1)
            for e in range(2):
                dve.wait_ge(inv_k_done, e + 1)
                link(nc.vector.transpose(
                    tmp3[:, 0, :].rearrange("p (k l) -> p l k", l=W)[:, e * W // 2:(e + 1) * W // 2],
                    ps[:, 4 + e, :].rearrange("p (o l) -> p l o", o=C)))
            for e in range(2):
                half = slice(e * HALF, (e + 1) * HALF)
                nc.vector.scalar_tensor_tensor(xb[:, half], tmp3[:, 0, half], 0.5 / HW, xc[:, half],
                                               ALU.mult, ALU.add).then_inc(res_ready, 1)

        @block.tensor
        def _(pe):
            mm = nc.tensor.matmul

            def keep_clock(bank, n):
                for _ in range(n):
                    mm(ps[:, bank, :], zeros[:, 0:P], zeros[:], start=True, stop=True)

            pe.wait_ge(zeros_ready, 1)
            pe.wait_ge(x_loaded[0], 16)
            keep_clock(7, 12)
            for n in (1, 3, 5, 6):
                pe.wait_ge(map_ready, n)
                keep_clock(7, 5)
            l0w = c_("l0w").rearrange("p (s o) -> p s o", o=32)
            pe.wait_ge(first_loaded, 16)
            for e in range(2):
                rows = [slice(32 * b, 32 * b + 32) for b in range(B)]
                for s, (t, (py, px)) in enumerate(SLOTS):
                    if t == 0:
                        if s == 0:
                            pe.wait_ge(tile_in[0] if e else tile0_top, B * 16)
                        for b in range(B):
                            last = mm(ps[rows[b], e, :].rearrange("p (y x) -> p y x", x=W), l0w[:, s, :],
                               window(stack[:, 0, b, :], py, px, 16 * e, 16, W), start=(s == 0), stop=False,
                               skip_group_check=True)
            last.then_inc(tile0_used, 1)
            for s, (t, (py, px)) in enumerate(SLOTS):
                if t == 0:
                    continue
                if SLOTS[s - 1][0] != t:
                    pe.wait_ge(tile_in[t], B * 16)
                for e in range(2):
                    for b in range(B):
                        last = mm(ps[32 * b:32 * b + 32, e, :].rearrange("p (y x) -> p y x", x=W), l0w[:, s, :],
                                  window(stack[:, t % 3, b, :], py, px, 16 * e, 16, W), start=False,
                                  stop=(s == len(SLOTS) - 1), skip_group_check=True)
            last.then_inc(l0_done, 1)

            pe.wait_ge(consts_loaded, 16)
            mm(ps[0:96, 7, 0:96], c_("ones", 0, 96)[:, 0:96], c_("l1w", 0, 96), start=True, stop=True
               ).then_inc(l1s_done, 1)
            keep_clock(6, 3)
            pe.wait_ge(l0_read, 1)
            keep_clock(6, 4)
            pe.wait_ge(l0_read, 2)
            keep_clock(6, 11)
            pe.wait_ge(padded, 2)
            for i in range(3):
                for r in range(3):
                    at = r * WP + i * PLANE
                    last = mm(ps[32 * r:32 * r + 32, 2 + i, 0:PLANE], c_("bsel"), xp[:, at:at + PLANE],
                              start=True, stop=True)
                last.then_inc(planes_done, 1)
            keep_clock(6, 3)
            pe.wait_ge(l1s_ready, 3)
            for e in range(2):
                pe.wait_ge(planes_ready, e + 2)
                for px in range(3):
                    last = mm(ps[:, e, :].rearrange("p (y x) -> p y x", x=W), l1s[:, px, :],
                              window(planes[0:96, :], 0, px, 16 * e, 16, W), start=(px == 0), stop=(px == 2))
                last.then_inc(l1_done, 1)

            keep_clock(6, 2)
            pe.wait_ge(l1_read, 2)
            keep_clock(6, 8)
            pe.wait_ge(padded, 3)
            for n in range(2 * B):
                e, b = divmod(n, B)
                for r in range(3):
                    last = mm(ps[32 * r:32 * r + 32, (2 + n) % 8, :].rearrange("p (y x) -> p y x", x=W),
                              c_("win")[:, 32 * b:32 * b + 32],
                              window(xp, r, 1, 16 * e, 16, W), start=True, stop=True)
                last.then_inc(xin_done, 1)

            def conv(bank, weights, rows, cols, first, signal):
                ny = rows // 2
                for e in range(2):
                    pe.wait_ge(xin_ready, e + 1)
                    for px in range(3):
                        for b in range(B):
                            last = mm(ps[32 * b:32 * b + 32, bank + e, 0:ny * cols].rearrange("p (y x) -> p y x", x=cols),
                                      weights[:, px, :],
                                      window(xst[:, b, :], first, first + px, ny * e, ny, cols),
                                      start=(px == 0), stop=(px == 2))
                    last.then_inc(signal, 1)

            qkv = c_("qkv").rearrange("p (a s o) -> p a s o", a=3, o=32)
            images = [slice(32 * b, 32 * b + 32) for b in range(B)]
            conv(2, qkv[:, 1], KH, KH, 1, k_done)
            pe.wait_ge(win_ready, 6)
            mm(ps[:, 0, 16:25], c_("win"), win9[:, 0, :], start=True, stop=True).then_inc(win_done, 1)
            conv(4, qkv[:, 0], H, W, 0, q_done)
            pe.wait_ge(win_scaled, 1)
            v2w = c_("v2w").rearrange("p (s o) -> p s o", o=32)
            for r in images:
                for s in range(9):
                    last = mm(ps[r, 0, 0:1], v2w[r, s, :], win9[r, 1, s:s + 1], start=(s == 0), stop=(s == 8))
            last.then_inc(a2_done, 1)
            conv(6, qkv[:, 2], KH, KH, 1, v_done)
            pe.wait_ge(a2_ready, 1)
            proj2 = c_("proj2").rearrange("p (s o) -> p s o", o=32)
            for r in images:
                for i in range(3):
                    last = mm(ps[r, 0, 8 + i:9 + i], proj2[r, i, :], a2[r, :], start=True, stop=True)
            last.then_inc(gb_done, 1)
            pe.wait_ge(vs_ready, 1)
            pe.wait_ge(gb_ready, 2)
            for t in range(DT):
                last = nc.tensor.transpose(ps[:, t // 4, (t % 4) * P:(t % 4 + 1) * P],
                                           vs[:, t * P:(t + 1) * P], c_("ident"))
                if t == 3:
                    last.then_inc(vt_done, 1)
            for h in range(HEADS):
                last = mm(ps[32 * h:32 * h + KREST, 1, 3 * P:4 * P], vs[:, DT * P:KEYS], c_("ident"),
                          start=True, stop=True)
            last.then_inc(vt_done, 1)

            def max_block(i, s, a, kind):
                before = block_before(i, block_bank(i))
                if before is not None:
                    pe.wait_ge(*blocks_read[before])
                e, b = divmod(s, B)
                h, qt = divmod(a, HALF_TILES)
                g = b * HEADS + h
                at = {"first": 0, "second": KHALF, "diff": KDIFF}[kind]
                mm(ps[:, block_bank(i), 0:KHALF], qst[:, e, g, qt * P:(qt + 1) * P], kst[:, g, at:at + KHALF],
                   start=True, stop=True).then_inc(max_scored, 1)

            def turn_maxima(i, s):
                pe.wait_ge(*blocks_read[block_before(i, block_bank(i))])
                pe.wait_ge(m_split, s + 1)
                nc.tensor.transpose(ps[0:PARTS * ROWS_OF_MAX, block_bank(i), 0:P // 2].bitcast(BF16),
                                    mparts[:].rearrange("p s n -> p (s n)"), ident_b[:]).then_inc(max_scored, 1)

            def score_tile(n):
                half, i = divmod(n, EXP_UNITS)
                e, b = divmod(half, B)
                if i == 0:
                    pe.wait_ge(m_in, 16 * (half + 1))
                bank = SCORE_RING[n % len(SCORE_RING)]
                if n >= len(SCORE_RING):
                    pe.wait_ge(expd, n - len(SCORE_RING) + 1)
                else:
                    pe.wait_ge(*blocks_read[block_before(prologue, bank)])
                if i < HEADS * DT:
                    t, h = divmod(i, HEADS)
                    g = b * HEADS + h
                    last = mm(ps[:, bank, :], kst[:, g, t * P:(t + 1) * P], qst[:, e, g, :],
                              start=True, stop=True)
                else:
                    for h in range(HEADS):
                        g = b * HEADS + h
                        last = mm(ps[32 * h:32 * h + 32, bank, :], kst[:, g, DT * P:KPAD],
                                  qst[:, e, g, :], start=True, stop=True)
                last.then_inc(scored, 1)

            def values(half, t):
                n0 = half * EXP_UNITS + t * HEADS
                bank = O_RING[half % len(O_RING)]
                if t == 0 and half >= len(O_RING):
                    pe.wait_ge(o_read, half - len(O_RING) + 1)
                if t < DT:
                    pe.wait_ge(expd, n0 + HEADS)
                    for h in range(HEADS):
                        last = mm(ps[32 * h:32 * h + 32, bank, :], vt[:, t, half % B * HEADS + h, :],
                                  probs[:, (n0 + h) % PRING, :], start=(t == 0), stop=False,
                                  skip_group_check=True)
                else:
                    pe.wait_ge(expd, n0 + 1)
                    last = mm(ps[:, bank, :], vrest[:, half % B, :], probs[:, n0 % PRING, :], start=False,
                              stop=True, skip_group_check=True)
                last.then_inc(pv_done, 1)

            proj = c_("proj").rearrange("p (s o) -> p s o", o=32)
            pe.wait_ge(q_part[2], 2)
            keep_clock(2, 3)
            pe.wait_ge(k_in[0], 16)
            pe.wait_ge(q_in[0], PARTS * 16)
            pe.wait_ge(vt_ready, 2 + HEADS)
            for item in plan:
                if item[0] == "max":
                    if item[2:5] == (0, ROWS_OF_MAX // 2, "diff"):
                        pe.wait_ge(k_in[1], 16)
                    elif item[2:5] == (1, 0, "diff"):
                        pe.wait_ge(k_in[2], 16)
                        pe.wait_ge(q_in[1], PARTS * 16)
                    elif item[2:5] == (B, 0, "diff"):
                        pe.wait_ge(q_in[2], PARTS * 16)
                    max_block(*item[1:])
                elif item[0] == "turn":
                    turn_maxima(*item[1:])
                elif item[0] == "score":
                    if item[1] == 0:
                        pe.wait_ge(vt_zeroed, 3 + HEADS)
                    score_tile(item[1])
                elif item[0] == "values":
                    values(*item[1:])

                elif item[0] == "gates":
                    p = item[1]
                    if p == 0:
                        for i in range(len(MAX_RING)):
                            pe.wait_ge(*blocks_read[turn_of[2 * B - 1] - i])
                    elif p == 1:
                        pe.wait_ge(x3_ready, 1)
                        keep_clock(6, 9)
                    else:
                        pe.wait_ge(expd, 2 * B * EXP_UNITS)
                    pe.wait_ge(attn_ready, B if p == 0 else 2 * B)
                    for i in range(3):
                        for b in range(B):
                            last = mm(piece_bank(GATE_BANKS[p][i], p)[32 * b:32 * b + 32], proj[:, i, :],
                                      attn[:, b, PIECES[p]], start=True, stop=True)
                        last.then_inc(gate_done, 1)
                elif item[0] == "out":
                    p = item[1]
                    if p > 0:
                        keep_clock(6, 4)
                    pe.wait_ge(h_ready, p + 1)
                    mm(piece_bank(OUT_BANKS[p], p), c_("wout"), tmp3[:, 5, PIECES[p]], start=True, stop=True
                       ).then_inc(wout_done, 1)

            pe.wait_ge(x3_ready, 3)
            keep_clock(7, 16)
            for i, m in enumerate(("mt", "mrt")):
                for e in range(2):
                    pe.wait_ge(t1_ready, e + 1)
                    last = mm(ps[:, 2 * i + e, :], c_(m), tmp3[:, 0, e * HALF:(e + 1) * HALF], start=True, stop=True)
                last.then_inc(rows_done, 1)
            for i, m in enumerate(("mt", "mrt")):
                pe.wait_ge(t2_ready, i + 1)
                src = tmp3[:, 1 + i, :].rearrange("p (c k) -> p c k", k=MODES)
                for b in range(B):
                    for g in range(4):
                        dst = ps[32 * g:32 * g + 32, 4 + 2 * i + b // 2, (b % 2) * 256:(b % 2 + 1) * 256]
                        last = mm(dst.rearrange("p (c k) -> p c k", k=KG), c_(m)[:, 32 * b:32 * b + 32],
                                  src[:, :, KG * g:KG * (g + 1)], start=True, stop=True)
                    if b % 2:
                        last.then_inc(cols_done, 1)
            keep_clock(3, 11)
            pe.wait_ge(wm_loaded, 16)
            xv = xm.rearrange("p (jh k l) m -> p k l jh m", jh=2, k=2)
            wv = wm.rearrange("p (jh k l m) -> p k l jh m", jh=2, k=2, m=2 * C)
            for i, (k2, lh) in enumerate(MODE_STAGES):
                pe.wait_ge(xm_dve, (i + 1) * (8 - POOL_MODES))
                pe.wait_ge(xm_pool, (i + 1) * POOL_MODES)
                for l in range(lh * MODES // 2, (lh + 1) * MODES // 2):
                    for jh in range(2):
                        last = mm(banks(4 * k2, 4)[64 * jh:64 * jh + 64, 64 * l:64 * l + 64], xv[:, k2, l, jh],
                                  wv[:, k2, l, jh], start=True, stop=True)
                if lh == 1:
                    last.then_inc(mix_done, 1)
            yv = y1.rearrange("p (k jl o g s b) -> p s b jl o g k", k=2, jl=2, o=C, g=4, s=2)
            pe.wait_ge(y1_ready, 2)
            keep_clock(0, 5)
            for s, m in enumerate(("mt", "mnt")):
                for jl in range(2):
                    pe.wait_ge(y1_ready, 3 + jl)
                    for jh in range(2):
                        j = 2 * jh + jl
                        zv = ps[:, 2 * s + jh, :].rearrange("p (o g k j) -> p j o g k", g=4, j=2, k=2)
                        for b in range(B):
                            last = mm(zv[32 * b:32 * b + 32, jl], c_(m)[:, 32 * j:32 * j + 32], yv[:, s, b, jl],
                                      start=(jl == 0), stop=True, skip_group_check=True)
                last.then_inc(inv_l_done, 1)
            for s in range(2):
                pe.wait_ge(z1_ready, s + 1)
                zs = z1[:, s * HW:(s + 1) * HW].rearrange("p (o l) -> p o l", l=W)
                for e in range(2):
                    last = mm(ps[:, 4 + e, :].rearrange("p (o l) -> p o l", o=C), c_(("mt_back", "mnt_back")[s]),
                              zs[:, :, e * W // 2:(e + 1) * W // 2], start=(s == 0), stop=(s == 1))
                    if s == 1:
                        last.then_inc(inv_k_done, 1)



def transform_matrix(n):
    if n == 1:
        return np.ones((1, 1), np.float32)
    m = transform_matrix(n // 2)
    k = np.arange(n // 2)
    cas = (np.cos(2 * np.pi * k / n) + np.sin(2 * np.pi * k / n)).astype(np.float32)[:, None]
    even = np.zeros((n // 2, n), np.float32)
    even[:, 0::2] = m
    odd = np.zeros((n // 2, n), np.float32)
    odd[:, 1::2] = m
    return np.concatenate([even + cas * odd, even - cas * odd], axis=0)


def blocks(m):
    out = np.zeros((P, P), np.float32)
    for b in range(B):
        out[32 * b:32 * b + 32, 32 * b:32 * b + 32] = m
    return out


def layout_consts(i):
    c = np.zeros((P, N_CONST), np.float32)

    def put(name, value, rows=P):
        at, n = CONSTS[name]
        c[0:rows, at:at + n] = np.asarray(value).reshape(rows, n)

    w1 = np.asarray(i["L0_conv_W1"]).reshape(C, 9, 32)
    w2 = np.asarray(i["L0_conv_W2"]).reshape(C, 9, 9, 32)
    l0 = np.zeros((C, 4, len(SLOTS), 32), np.float32)
    for s, (t, (py, px)) in enumerate(SLOTS):
        for slot, (d, pre) in enumerate(TILES[t][0]):
            pair = tap_pair(d, pre, py, px)
            if pair:
                l0[:, slot, s, :] = w1[:, pair[0]] if d is LINEAR else w2[:, pair[0], pair[1]]
    put("l0w", l0)
    put("l0bias", np.tile(np.asarray(i["L0_conv_bias_w"]).reshape(32), B))
    put("l1w", np.asarray(i["L1_conv_weight"])[:, :, ::-1, ::-1].transpose(2, 1, 3, 0), 96)
    bsel = np.zeros((B, C, 32), np.float32)
    dmask = np.zeros((4, 32, B), np.float32)
    for b in range(B):
        bsel[b, :, b] = 1
        dmask[:, b, b] = 1
    put("bsel", bsel)
    put("dmask", dmask)
    put("ones", blocks(np.ones((32, 32), np.float32)))
    put("l1bias", np.tile(np.asarray(i["L1_conv_bias"]), B))
    put("win", blocks(np.asarray(i["L2_conv_W_in"]).T))
    put("bin", np.tile(np.asarray(i["L2_conv_b_in"]), B))
    qkv = np.stack([np.asarray(i["L2_conv_" + n])[0] for n in ("Wq", "Wk", "Wv")])
    put("qkv", qkv.transpose(3, 2, 0, 4, 1), 96)
    put("v2w", np.tile(np.asarray(i["L2_conv_Wv"])[2].reshape(32, C, 9).transpose(1, 2, 0), (B, 1, 1)))
    wproj = np.asarray(i["L2_conv_Wproj"])[list(GATES)]
    proj = np.zeros((HEADS, 32, 3, 32), np.float32)
    proj[:, 0:HC] = wproj[:, 0].reshape(3, 32, HEADS, HC).transpose(2, 3, 0, 1)
    put("proj", proj)
    put("proj2", np.tile(wproj[:, 2].transpose(2, 0, 1), (B, 1, 1)))
    put("gbias", np.tile(np.asarray(i["L2_conv_b_gates"])[list(GATES)].T, (B, 1)))
    put("wout", blocks(np.asarray(i["L2_conv_W_out"]).T))
    put("bout", np.tile(np.asarray(i["L2_conv_b_out"]), B))
    put("ident", np.eye(P, dtype=np.float32))
    m = transform_matrix(MODES)
    neg = -np.arange(MODES) % MODES
    put("mt", blocks(m.T))
    put("mrt", blocks(m[neg].T))
    put("mnt", blocks(m[:, neg].T))
    order = np.arange(MODES).reshape(4, 2, 4).transpose(1, 0, 2).reshape(-1)
    put("mt_back", blocks(m.T[order]))
    put("mnt_back", blocks(m[:, neg].T[order]))
    return c


def kernel(**inputs):
    import concourse.bacc as bacc
    from concourse.bass_utils import run_bass_kernel_spmd

    wmodes = np.asarray(inputs["L3_conv_weights1"]).reshape(C, 32, 4, KG // 2, 2, MODES)
    wmodes = wmodes.transpose(2, 0, 3, 5, 4, 1).reshape(P, KG * MODES * 32)
    arrays = {"x": np.ascontiguousarray(np.asarray(inputs["x"]).reshape(P, HW)),
              "consts": layout_consts(inputs), "wmodes": np.ascontiguousarray(wmodes)}
    nc = bacc.Bacc("TRN2", target_bir_lowering=False, num_devices=1)
    args = [nc.dram_tensor(n, a.shape, F32, kind="ExternalInput").ap() for n, a in arrays.items()]
    out = nc.dram_tensor("out", [P, HW], F32, kind="ExternalOutput").ap()
    build(nc, *args, out)
    r = run_bass_kernel_spmd(nc, [arrays], core_ids=[0])
    return r.results[0]["out"].reshape(B, C, H, W)
```
